# Optimizing a Trainium2 kernel written in Bass

```python
import numpy as np
import jax
import jax.numpy as jnp

def _softmax(x, axis=-1):
    return jax.nn.softmax(x, axis=axis)

def _gelu(x):
    return jax.nn.gelu(x, approximate=True)

def _silu(x):
    return jax.nn.silu(x)

def _sigmoid(x):
    return jax.nn.sigmoid(x)

def _layernorm(x, axis=-1, eps=1e-05):
    m = jnp.mean(x, axis=axis, keepdims=True)
    v = jnp.var(x, axis=axis, keepdims=True)
    return (x - m) / jnp.sqrt(v + eps)

def _scatter_add(tgt, idx, src, axis=0):
    return tgt.at[idx].add(src)

def _segment_sum(src, seg, n):
    return jax.ops.segment_sum(src, seg, n)
kernel_name = 'mk_xattn_seq_d2_seqx_r8_6b010e'

def setup_inputs(seed: int=0):
    np.random.seed(seed)
    _w = jnp.asarray

    def _rec_inputs():
        import jax
        import jax.numpy as jnp
        _rk = jax.random.key(seed)
        x = -0.0001233 + 1 * jax.random.normal(jax.random.fold_in(_rk, 1), (64, 128, 160), jnp.float32)
        _lenS = 128 - jax.random.randint(jax.random.fold_in(_rk, 7), (64,), 0, max(1, 128 // 4) + 1, jnp.int32)
        _lenS2 = 77 - jax.random.randint(jax.random.fold_in(_rk, 8), (64,), 0, max(1, 77 // 4) + 1, jnp.int32)
        _ctx_768P = jax.random.normal(jax.random.fold_in(_rk, 11), (64, 16, 96), jnp.float32)
        _ctx_768c = jax.random.dirichlet(jax.random.fold_in(_rk, 511), 0.3 * jnp.ones((16,), jnp.float32), (64, 77))
        _ctx_768t = jnp.einsum('bsk,bkd->bsd', _ctx_768c, _ctx_768P)
        _ctx_768t = _ctx_768t * jax.lax.rsqrt(jnp.mean(jnp.square(_ctx_768t)) + 1e-12) * 0.953939
        ctx_768 = 0.00272024 + 0.999456 * (_ctx_768t + 0.3 * jax.random.normal(jax.random.fold_in(_rk, 611), (64, 77, 96), jnp.float32))
        return (x, ctx_768)
    x, ctx_768 = _rec_inputs()

    def _L0_xattn_setup():
        import jax, jax.numpy as jnp
        import numpy as np
        D = 160
        H = 20
        DH = D // H
        CTX = 96
        FF_IN = 4 * D
        EPS = 1e-05

        def _ln(x, g, b):
            m = jnp.mean(x, axis=-1, keepdims=True)
            v = jnp.mean(jnp.square(x - m), axis=-1, keepdims=True)
            return (x - m) * jax.lax.rsqrt(v + EPS) * g + b

        def _attn(x, ctx, wq, wk, wv, wo, bo, heads):
            b, n, _ = x.shape
            j = ctx.shape[1]
            dh = wq.shape[1] // heads
            scale = dh ** (-0.5)
            q = (x @ wq).reshape(b, n, heads, dh).transpose(0, 2, 1, 3)
            k = (ctx @ wk).reshape(b, j, heads, dh).transpose(0, 2, 1, 3)
            v = (ctx @ wv).reshape(b, j, heads, dh).transpose(0, 2, 1, 3)
            sim = jnp.einsum('bhid,bhjd->bhij', q, k) * scale
            a = jax.nn.softmax(sim, axis=-1)
            out = jnp.einsum('bhij,bhjd->bhid', a, v)
            out = out.transpose(0, 2, 1, 3).reshape(b, n, heads * dh)
            return out @ wo + bo
        key = jax.random.key(seed)
        ks = jax.random.split(key, 24)
        r = lambda k, shp, s: jax.random.normal(k, shp, dtype=jnp.float32) * s
        d = {'x': r(ks[0], (8, 128, D), 1.0), 'context': r(ks[1], (8, 77, CTX), 1.0), 'heads': H, 'n1_g': jnp.ones((D,), jnp.float32), 'n1_b': jnp.zeros((D,), jnp.float32), 'q1': r(ks[2], (D, D), D ** (-0.5)), 'k1': r(ks[3], (D, D), D ** (-0.5)), 'v1': r(ks[4], (D, D), D ** (-0.5)), 'o1_w': r(ks[5], (D, D), D ** (-0.5)), 'o1_b': jnp.zeros((D,), jnp.float32), 'n2_g': jnp.ones((D,), jnp.float32), 'n2_b': jnp.zeros((D,), jnp.float32), 'q2': r(ks[6], (D, D), D ** (-0.5)), 'k2': r(ks[7], (CTX, D), CTX ** (-0.5)), 'v2': r(ks[8], (CTX, D), CTX ** (-0.5)), 'o2_w': r(ks[9], (D, D), D ** (-0.5)), 'o2_b': jnp.zeros((D,), jnp.float32), 'n3_g': jnp.ones((D,), jnp.float32), 'n3_b': jnp.zeros((D,), jnp.float32), 'ff_w1': r(ks[10], (D, 2 * FF_IN), D ** (-0.5)), 'ff_b1': jnp.zeros((2 * FF_IN,), jnp.float32), 'ff_w2': r(ks[11], (FF_IN, D), FF_IN ** (-0.5)), 'ff_b2': jnp.zeros((D,), jnp.float32)}
        return d
    _L0_xattn_all = _L0_xattn_setup()
    _L0_xattn_in = {k: v for k, v in _L0_xattn_all.items() if k in ('n1_g', 'n1_b', 'q1', 'k1', 'v1', 'o1_w', 'o1_b', 'n2_g', 'n2_b', 'q2', 'k2', 'v2', 'o2_w', 'o2_b', 'n3_g', 'n3_b', 'ff_w1', 'ff_b1', 'ff_w2', 'ff_b2')}
    del _L0_xattn_all

    def _L1_xattn_setup():
        import jax, jax.numpy as jnp
        import numpy as np
        DIM, HEADS, DHEAD, CTX_DIM, DFF = (160, 20, 64, 96, 640)
        EPS = 1e-05
        SCALE = DHEAD ** (-0.5)

        def layer_norm(x, g, b):
            mu = jnp.mean(x, axis=-1, keepdims=True)
            var = jnp.mean(jnp.square(x - mu), axis=-1, keepdims=True)
            return (x - mu) * jax.lax.rsqrt(var + EPS) * g + b

        def cross_attention(x, ctx, wq, wk, wv, wo, bo):
            B, N, _ = x.shape
            M = ctx.shape[1]
            q = jnp.einsum('bne,ef->bnf', x, wq).reshape(B, N, HEADS, DHEAD).transpose(0, 2, 1, 3)
            k = jnp.einsum('bme,ef->bmf', ctx, wk).reshape(B, M, HEADS, DHEAD).transpose(0, 2, 1, 3)
            v = jnp.einsum('bme,ef->bmf', ctx, wv).reshape(B, M, HEADS, DHEAD).transpose(0, 2, 1, 3)
            scores = jnp.einsum('bhnd,bhmd->bhnm', q, k) * SCALE
            attn = jax.nn.softmax(scores, axis=-1)
            out = jnp.einsum('bhnm,bhmd->bhnd', attn, v)
            out = out.transpose(0, 2, 1, 3).reshape(B, N, HEADS * DHEAD)
            return jnp.einsum('bnf,fe->bne', out, wo) + bo

        def geglu_ff(x, w1, b1, w2, b2):
            h = jnp.einsum('bne,ef->bnf', x, w1) + b1
            a, gate = (h[..., :DFF], h[..., DFF:])
            h = a * jax.nn.gelu(gate)
            return jnp.einsum('bnf,fe->bne', h, w2) + b2

        def block_forward(x, context, g1, be1, wq1, wk1, wv1, wo1, bo1, g2, be2, wq2, wk2, wv2, wo2, bo2, g3, be3, w_ff1, b_ff1, w_ff2, b_ff2):
            x = cross_attention(layer_norm(x, g1, be1), layer_norm(x, g1, be1), wq1, wk1, wv1, wo1, bo1) + x
            x = cross_attention(layer_norm(x, g2, be2), context, wq2, wk2, wv2, wo2, bo2) + x
            return geglu_ff(layer_norm(x, g3, be3), w_ff1, b_ff1, w_ff2, b_ff2) + x
        key = jax.random.key(seed)
        ks = jax.random.split(key, 20)
        s = 0.02
        inner = HEADS * DHEAD
        return {'x': jax.random.normal(ks[0], (4, 128, DIM), jnp.float32), 'context': jax.random.normal(ks[1], (4, 77, CTX_DIM), jnp.float32), 'g1': jnp.ones((DIM,), jnp.float32), 'be1': jnp.zeros((DIM,), jnp.float32), 'wq1': jax.random.normal(ks[2], (DIM, inner), jnp.float32) * s, 'wk1': jax.random.normal(ks[3], (DIM, inner), jnp.float32) * s, 'wv1': jax.random.normal(ks[4], (DIM, inner), jnp.float32) * s, 'wo1': jax.random.normal(ks[5], (inner, DIM), jnp.float32) * s, 'bo1': jnp.zeros((DIM,), jnp.float32), 'g2': jnp.ones((DIM,), jnp.float32), 'be2': jnp.zeros((DIM,), jnp.float32), 'wq2': jax.random.normal(ks[6], (DIM, inner), jnp.float32) * s, 'wk2': jax.random.normal(ks[7], (CTX_DIM, inner), jnp.float32) * s, 'wv2': jax.random.normal(ks[8], (CTX_DIM, inner), jnp.float32) * s, 'wo2': jax.random.normal(ks[9], (inner, DIM), jnp.float32) * s, 'bo2': jnp.zeros((DIM,), jnp.float32), 'g3': jnp.ones((DIM,), jnp.float32), 'be3': jnp.zeros((DIM,), jnp.float32), 'w_ff1': jax.random.normal(ks[10], (DIM, 2 * DFF), jnp.float32) * s, 'b_ff1': jnp.zeros((2 * DFF,), jnp.float32), 'w_ff2': jax.random.normal(ks[11], (DFF, DIM), jnp.float32) * s, 'b_ff2': jnp.zeros((DIM,), jnp.float32)}
    _L1_xattn_all = _L1_xattn_setup()
    _L1_xattn_in = {k: v for k, v in _L1_xattn_all.items() if k in ('g1', 'be1', 'wq1', 'wk1', 'wv1', 'wo1', 'bo1', 'g2', 'be2', 'wq2', 'wk2', 'wv2', 'wo2', 'bo2', 'g3', 'be3', 'w_ff1', 'b_ff1', 'w_ff2', 'b_ff2')}
    del _L1_xattn_all
    return {'x': x, 'ctx_768': ctx_768, 'L0_xattn_n1_g': _L0_xattn_in['n1_g'], 'L0_xattn_n1_b': _L0_xattn_in['n1_b'], 'L0_xattn_q1': _L0_xattn_in['q1'], 'L0_xattn_k1': _L0_xattn_in['k1'], 'L0_xattn_v1': _L0_xattn_in['v1'], 'L0_xattn_o1_w': _L0_xattn_in['o1_w'], 'L0_xattn_o1_b': _L0_xattn_in['o1_b'], 'L0_xattn_n2_g': _L0_xattn_in['n2_g'], 'L0_xattn_n2_b': _L0_xattn_in['n2_b'], 'L0_xattn_q2': _L0_xattn_in['q2'], 'L0_xattn_k2': _L0_xattn_in['k2'], 'L0_xattn_v2': _L0_xattn_in['v2'], 'L0_xattn_o2_w': _L0_xattn_in['o2_w'], 'L0_xattn_o2_b': _L0_xattn_in['o2_b'], 'L0_xattn_n3_g': _L0_xattn_in['n3_g'], 'L0_xattn_n3_b': _L0_xattn_in['n3_b'], 'L0_xattn_ff_w1': _L0_xattn_in['ff_w1'], 'L0_xattn_ff_b1': _L0_xattn_in['ff_b1'], 'L0_xattn_ff_w2': _L0_xattn_in['ff_w2'], 'L0_xattn_ff_b2': _L0_xattn_in['ff_b2'], 'L1_xattn_g1': _L1_xattn_in['g1'], 'L1_xattn_be1': _L1_xattn_in['be1'], 'L1_xattn_wq1': _L1_xattn_in['wq1'], 'L1_xattn_wk1': _L1_xattn_in['wk1'], 'L1_xattn_wv1': _L1_xattn_in['wv1'], 'L1_xattn_wo1': _L1_xattn_in['wo1'], 'L1_xattn_bo1': _L1_xattn_in['bo1'], 'L1_xattn_g2': _L1_xattn_in['g2'], 'L1_xattn_be2': _L1_xattn_in['be2'], 'L1_xattn_wq2': _L1_xattn_in['wq2'], 'L1_xattn_wk2': _L1_xattn_in['wk2'], 'L1_xattn_wv2': _L1_xattn_in['wv2'], 'L1_xattn_wo2': _L1_xattn_in['wo2'], 'L1_xattn_bo2': _L1_xattn_in['bo2'], 'L1_xattn_g3': _L1_xattn_in['g3'], 'L1_xattn_be3': _L1_xattn_in['be3'], 'L1_xattn_w_ff1': _L1_xattn_in['w_ff1'], 'L1_xattn_b_ff1': _L1_xattn_in['b_ff1'], 'L1_xattn_w_ff2': _L1_xattn_in['w_ff2'], 'L1_xattn_b_ff2': _L1_xattn_in['b_ff2']}

def reference(x, ctx_768, L0_xattn_n1_g, L0_xattn_n1_b, L0_xattn_q1, L0_xattn_k1, L0_xattn_v1, L0_xattn_o1_w, L0_xattn_o1_b, L0_xattn_n2_g, L0_xattn_n2_b, L0_xattn_q2, L0_xattn_k2, L0_xattn_v2, L0_xattn_o2_w, L0_xattn_o2_b, L0_xattn_n3_g, L0_xattn_n3_b, L0_xattn_ff_w1, L0_xattn_ff_b1, L0_xattn_ff_w2, L0_xattn_ff_b2, L1_xattn_g1, L1_xattn_be1, L1_xattn_wq1, L1_xattn_wk1, L1_xattn_wv1, L1_xattn_wo1, L1_xattn_bo1, L1_xattn_g2, L1_xattn_be2, L1_xattn_wq2, L1_xattn_wk2, L1_xattn_wv2, L1_xattn_wo2, L1_xattn_bo2, L1_xattn_g3, L1_xattn_be3, L1_xattn_w_ff1, L1_xattn_b_ff1, L1_xattn_w_ff2, L1_xattn_b_ff2):
    import jax
    import jax.numpy as jnp

    def _L0_xattn_ref(x, context, heads, n1_g, n1_b, q1, k1, v1, o1_w, o1_b, n2_g, n2_b, q2, k2, v2, o2_w, o2_b, n3_g, n3_b, ff_w1, ff_b1, ff_w2, ff_b2):
        import jax, jax.numpy as jnp
        import numpy as np
        D = 160
        H = 20
        DH = D // H
        CTX = 96
        FF_IN = 4 * D
        EPS = 1e-05

        def _ln(x, g, b):
            m = jnp.mean(x, axis=-1, keepdims=True)
            v = jnp.mean(jnp.square(x - m), axis=-1, keepdims=True)
            return (x - m) * jax.lax.rsqrt(v + EPS) * g + b

        def _attn(x, ctx, wq, wk, wv, wo, bo, heads):
            b, n, _ = x.shape
            j = ctx.shape[1]
            dh = wq.shape[1] // heads
            scale = dh ** (-0.5)
            q = (x @ wq).reshape(b, n, heads, dh).transpose(0, 2, 1, 3)
            k = (ctx @ wk).reshape(b, j, heads, dh).transpose(0, 2, 1, 3)
            v = (ctx @ wv).reshape(b, j, heads, dh).transpose(0, 2, 1, 3)
            sim = jnp.einsum('bhid,bhjd->bhij', q, k) * scale
            a = jax.nn.softmax(sim, axis=-1)
            out = jnp.einsum('bhij,bhjd->bhid', a, v)
            out = out.transpose(0, 2, 1, 3).reshape(b, n, heads * dh)
            return out @ wo + bo
        h1 = _ln(x, n1_g, n1_b)
        x = _attn(h1, h1, q1, k1, v1, o1_w, o1_b, heads) + x
        h2 = _ln(x, n2_g, n2_b)
        x = _attn(h2, context, q2, k2, v2, o2_w, o2_b, heads) + x
        h3 = _ln(x, n3_g, n3_b)
        proj = h3 @ ff_w1 + ff_b1
        a, g = jnp.split(proj, 2, axis=-1)
        ff = a * jax.nn.gelu(g, approximate=False) @ ff_w2 + ff_b2
        return ff + x

    def _L1_xattn_ref(x, context, g1, be1, wq1, wk1, wv1, wo1, bo1, g2, be2, wq2, wk2, wv2, wo2, bo2, g3, be3, w_ff1, b_ff1, w_ff2, b_ff2):
        import jax, jax.numpy as jnp
        import numpy as np
        DIM, HEADS, DHEAD, CTX_DIM, DFF = (160, 20, 64, 96, 640)
        EPS = 1e-05
        SCALE = DHEAD ** (-0.5)

        def layer_norm(x, g, b):
            mu = jnp.mean(x, axis=-1, keepdims=True)
            var = jnp.mean(jnp.square(x - mu), axis=-1, keepdims=True)
            return (x - mu) * jax.lax.rsqrt(var + EPS) * g + b

        def cross_attention(x, ctx, wq, wk, wv, wo, bo):
            B, N, _ = x.shape
            M = ctx.shape[1]
            q = jnp.einsum('bne,ef->bnf', x, wq).reshape(B, N, HEADS, DHEAD).transpose(0, 2, 1, 3)
            k = jnp.einsum('bme,ef->bmf', ctx, wk).reshape(B, M, HEADS, DHEAD).transpose(0, 2, 1, 3)
            v = jnp.einsum('bme,ef->bmf', ctx, wv).reshape(B, M, HEADS, DHEAD).transpose(0, 2, 1, 3)
            scores = jnp.einsum('bhnd,bhmd->bhnm', q, k) * SCALE
            attn = jax.nn.softmax(scores, axis=-1)
            out = jnp.einsum('bhnm,bhmd->bhnd', attn, v)
            out = out.transpose(0, 2, 1, 3).reshape(B, N, HEADS * DHEAD)
            return jnp.einsum('bnf,fe->bne', out, wo) + bo

        def geglu_ff(x, w1, b1, w2, b2):
            h = jnp.einsum('bne,ef->bnf', x, w1) + b1
            a, gate = (h[..., :DFF], h[..., DFF:])
            h = a * jax.nn.gelu(gate)
            return jnp.einsum('bnf,fe->bne', h, w2) + b2

        def block_forward(x, context, g1, be1, wq1, wk1, wv1, wo1, bo1, g2, be2, wq2, wk2, wv2, wo2, bo2, g3, be3, w_ff1, b_ff1, w_ff2, b_ff2):
            x = cross_attention(layer_norm(x, g1, be1), layer_norm(x, g1, be1), wq1, wk1, wv1, wo1, bo1) + x
            x = cross_attention(layer_norm(x, g2, be2), context, wq2, wk2, wv2, wo2, bo2) + x
            return geglu_ff(layer_norm(x, g3, be3), w_ff1, b_ff1, w_ff2, b_ff2) + x
        return block_forward(x, context, g1, be1, wq1, wk1, wv1, wo1, bo1, g2, be2, wq2, wk2, wv2, wo2, bo2, g3, be3, w_ff1, b_ff1, w_ff2, b_ff2)
    x = _L0_xattn_ref(x, ctx_768, 20, L0_xattn_n1_g, L0_xattn_n1_b, L0_xattn_q1, L0_xattn_k1, L0_xattn_v1, L0_xattn_o1_w, L0_xattn_o1_b, L0_xattn_n2_g, L0_xattn_n2_b, L0_xattn_q2, L0_xattn_k2, L0_xattn_v2, L0_xattn_o2_w, L0_xattn_o2_b, L0_xattn_n3_g, L0_xattn_n3_b, L0_xattn_ff_w1, L0_xattn_ff_b1, L0_xattn_ff_w2, L0_xattn_ff_b2)
    x = _L1_xattn_ref(x, ctx_768, L1_xattn_g1, L1_xattn_be1, L1_xattn_wq1, L1_xattn_wk1, L1_xattn_wv1, L1_xattn_wo1, L1_xattn_bo1, L1_xattn_g2, L1_xattn_be2, L1_xattn_wq2, L1_xattn_wk2, L1_xattn_wv2, L1_xattn_wo2, L1_xattn_bo2, L1_xattn_g3, L1_xattn_be3, L1_xattn_w_ff1, L1_xattn_b_ff1, L1_xattn_w_ff2, L1_xattn_b_ff2)
    return x

_drawn_inputs = setup_inputs


def setup_inputs(seed=0):
    import zlib

    import numpy as np

    out = dict(_drawn_inputs(seed))
    spreads = {'L0_xattn_n1_g': (1.0, 0.2),
     'L0_xattn_n1_b': (0.0, 0.1),
     'L0_xattn_o1_b': (0.0, 0.1),
     'L0_xattn_n2_g': (1.0, 0.2),
     'L0_xattn_n2_b': (0.0, 0.355),
     'L0_xattn_o2_b': (0.0, 0.1),
     'L0_xattn_n3_g': (1.0, 0.2),
     'L0_xattn_n3_b': (0.0, 0.1),
     'L0_xattn_ff_b1': (0.0, 0.1),
     'L0_xattn_ff_b2': (0.0, 0.1),
     'L1_xattn_g1': (1.0, 0.6),
     'L1_xattn_be1': (0.0, 0.509),
     'L1_xattn_bo1': (0.0, 0.1),
     'L1_xattn_g2': (1.0, 0.6),
     'L1_xattn_be2': (0.0, 0.8),
     'L1_xattn_bo2': (0.0, 0.1),
     'L1_xattn_g3': (1.0, 0.6),
     'L1_xattn_be3': (0.0, 0.8),
     'L1_xattn_b_ff1': (0.0, 0.8),
     'L1_xattn_b_ff2': (0.0, 0.323)}
    factors = {'L1_xattn_wq1': 8.0,
     'L1_xattn_wk1': 8.0,
     'L1_xattn_wq2': 8.0,
     'L1_xattn_wk2': 8.0,
     'L1_xattn_w_ff1': 3.568,
     'L1_xattn_w_ff2': 3.527}
    for name, (base, spread) in spreads.items():
        noise = np.random.default_rng([zlib.crc32(name.encode()), seed]).standard_normal(out[name].shape)
        drawn = base * np.exp(spread * noise) if base else spread * noise
        out[name] = jnp.asarray(drawn.astype(out[name].dtype))
    for name, factor in factors.items():
        out[name] = (out[name] * factor).astype(out[name].dtype)
    return out
```

```python
import numpy as np
import concourse.bass as bass
from concourse import mybir
from contextlib import ExitStack

F32 = mybir.dt.float32
F32R = mybir.dt.float32r
ALU = mybir.AluOpType
ACT = mybir.ActivationFunctionType
AX = mybir.AxisListType

P = 128
SEQS, TOK, D = 64, 128, 160
CTX_TOK, CTX_D = 77, 96
HEADS = 20
FF = 640
MAIN = 128
REM = D - MAIN
STACK = 3 * REM
GROUP = 4
GROUPS = HEADS // GROUP
PAIR = 2
PSTEPS = PAIR * GROUPS
QSTEPS = 2 * PSTEPS
PAIRS = SEQS // PAIR
QUADS = SEQS // (2 * PAIR)
STEPS = SEQS * GROUPS
EPS = 1e-5


def live(value, total):
    return not isinstance(value, int) or 0 <= value < total


def due(count):
    return not isinstance(count, int) or count > 0


def address(engine, value):
    return value if isinstance(value, int) else engine.snap(value)


def clear(nc, semaphores):
    with nc.Block() as block:
        @block.sync
        def _(sp):
            for semaphore in semaphores:
                sp.sem_clear(semaphore)


class Machine:

    def __init__(self, nc):
        self.nc, self.stage_semaphores = nc, []

    def semaphore(self, ctx, name):
        self.stage_semaphores.append(ctx.enter_context(self.nc.semaphore(name)))
        return self.stage_semaphores[-1]

    def end_stage(self):
        clear(self.nc, self.stage_semaphores)
        self.stage_semaphores = []


class Norm:

    def __init__(self, m, ctx, tag, bank, done_reading):
        nc = m.nc
        sb = lambda name, shape, dt=F32: ctx.enter_context(nc.sbuf_tensor(f"{tag}_{name}", shape, dt))
        sem = lambda name: m.semaphore(ctx, f"{tag}_{name}")
        self.m, self.bank, self.done_reading = m, bank, done_reading
        self.stats = sb("stats", [P, PAIR, 6])
        self.moments = sb("moments", [P, PAIR, 2])
        self.var_eps = sb("var_eps", [P, PAIR])
        self.rstd = sb("rstd", [P, PAIR])
        self.h = sb("h", [P, PAIR, 2 * P])
        self.y = sb("y", [P, 2, PAIR * P])
        self.yhigh = sb("yhigh", [P, PAIR * P], F32R)
        self.high = [sb(f"high{i}", [P, PAIR * P], F32R) for i in range(2)]
        self.low = [sb(f"low{i}", [P, PAIR * P], F32R) for i in range(2)]
        self.stack = [sb(f"stack{i}", [P, PAIR * P], F32R) for i in range(2)]
        self.s_stats6 = sem("stats6")
        self.s_moments = sem("moments_ready")
        self.s_vareps = sem("var_eps_ready")
        self.s_rstd = sem("rstd_ready")
        self.s_h = sem("h_ready")
        self.s_biased = sem("x_biased")
        self.s_hT = sem("hT_ready")
        self.s_y = sem("y_ready")
        self.s_high = sem("high_ready")
        self.s_split = sem("split_ready")

    def vector_stats(self, e, n, seq):
        nc, m = self.m.nc, self.m
        if due(n):
            e.wait_ge(self.s_h, n)
        for a in range(PAIR):
            nc.vector.bn_stats(self.stats[:, a, :], m.xs(seq, a)).then_inc(self.s_stats6, 1)

    def wait_stats(self, e, n):
        if due(n * PAIR + PAIR):
            e.wait_ge(self.s_stats6, n * PAIR + PAIR)

    def vector_moments(self, e, n):
        for a in range(PAIR):
            self.m.nc.vector.bn_aggr(self.moments[:, a, :], self.stats[:, a, :]).then_inc(self.s_moments, 1)

    def gpsimd_rstd(self, e, n):
        nc = self.m.nc
        if due(n * PAIR + PAIR):
            e.wait_ge(self.s_moments, n * PAIR + PAIR)
        nc.gpsimd.tensor_tensor(self.var_eps[:], self.moments[:, :, 1], self.m.eps[:], ALU.add).then_inc(self.s_vareps, 1)
        if due(n + 1):
            e.wait_ge(self.s_vareps, n + 1)
        nc.gpsimd.tensor_tensor(self.rstd[:], self.var_eps[:], self.m.minus_half[:], ALU.pow).then_inc(self.s_rstd, 1)

    def vector_h(self, e, n, seq):
        nc, m = self.m.nc, self.m
        if due(n + 1):
            e.wait_ge(self.s_rstd, n + 1)
        if due(n):
            e.wait_ge(self.s_hT, n)
        for a in range(PAIR):
            mean, rstd = self.moments[:, a, 0:1], self.rstd[:, a:a + 1]
            nc.vector.tensor_scalar(self.h[:, a, 0:MAIN], m.xs(seq, a)[:, 0:MAIN], mean, rstd, ALU.subtract, ALU.mult)
            last = nc.vector.tensor_scalar(
                self.h[:, a, MAIN:].rearrange("p (c d) -> p c d", d=REM),
                m.xs(seq, a)[:, MAIN:D].unsqueeze(1).broadcast_to([P, 4, REM]), mean, rstd, ALU.subtract, ALU.mult)
        last.then_inc(self.s_h, 1)

    def gpsimd_bias(self, e, n, seq):
        nc, m = self.m.nc, self.m
        if due(n + 1):
            e.wait_ge(self.s_h, n + 1)
        nc.gpsimd.tensor_tensor(m.xpair(seq), m.xpair(seq), m.out_bias[:].unsqueeze(1).broadcast_to([P, PAIR, D]),
                                ALU.add).then_inc(self.s_biased, 1)

    def tensor_transpose(self, e, n):
        nc = self.m.nc
        if due(n + 1):
            e.wait_ge(self.s_h, n + 1)
        if due(n * 2):
            e.wait_ge(self.s_y, n * 2)
        used, count = self.done_reading(n)
        if due(count):
            e.wait_ge(used, count)
        for part in range(2):
            for a in range(PAIR):
                last = nc.tensor.transpose(self.bank[:, part * PAIR * P + a * P: part * PAIR * P + (a + 1) * P],
                                           self.h[:, a, part * P:(part + 1) * P], self.m.ident[:])
        last.then_inc(self.s_hT, 1)

    def scalar_affine(self, e, n, par, parts_used):
        nc, m = self.m.nc, self.m
        if due(n + 1):
            e.wait_ge(self.s_hT, n + 1)
        if due(n):
            e.wait_ge(self.s_split, n)
        for part in range(2):
            nc.scalar.activation(self.y[:, part, :], self.bank[:, part * PAIR * P:(part + 1) * PAIR * P], ACT.Identity,
                                 bias=m.norm_cols[:, 2 * part + 1:2 * part + 2],
                                 scale=m.norm_cols[:, 2 * part:2 * part + 1]).then_inc(self.s_y, 1)
        if due(n * 2 + 2):
            e.wait_ge(self.s_y, n * 2 + 2)
        used, count = parts_used
        if due(count):
            e.wait_ge(used, count)
        nc.scalar.copy(self.high[par][:], self.y[:, 0, :]).then_inc(self.s_high, 1)
        nc.scalar.copy(self.yhigh[:], self.y[:, 1, :]).then_inc(self.s_high, 1)

    def vector_split(self, e, n, par):
        nc, m = self.m.nc, self.m
        if due(n * 2 + 2):
            e.wait_ge(self.s_high, n * 2 + 2)
        nc.vector.tensor_tensor(self.low[par][:], self.y[:, 0, :], self.high[par][:].bitcast(F32), ALU.subtract)
        nc.vector.scalar_tensor_tensor(out=self.stack[par][:], in0=self.yhigh[:].bitcast(F32), scalar=m.minus_low_row[:, 0:1],
                                       in1=self.y[:, 1, :], op0=ALU.mult, op1=ALU.add).then_inc(self.s_split, 1)


def prepare_weights(m, tag, jobs, extra_loads, fills=()):
    nc = m.nc
    with ExitStack() as ctx:
        sb = lambda name, shape, dt=F32: ctx.enter_context(nc.sbuf_tensor(f"{tag}_{name}", shape, dt))
        sem = lambda name: m.semaphore(ctx, f"{tag}_{name}")
        WIDE = 1280
        plain = [sb(f"plain{i}", [P, WIDE]) for i in range(2)]
        plain_rem = [sb(f"plain_rem{i}", [P, WIDE]) for i in range(2)]
        scaled = sb("scaled", [P, WIDE])
        scaled_rem = sb("scaled_rem", [P, WIDE])
        rem_high = sb("rem_high", [P, WIDE], F32R)
        s_load = [sem(f"load{i}") for i in range(len(jobs))]
        s_extra = sem("extra")
        s_job = sem("job")
        s_link = sem("link")
        s_fill = sem("fill")
        ctx.callback(m.end_stage)
        block = ctx.enter_context(nc.Block())

        @block.sync
        def _(sp):
            for i, (src, parts, cols, scale, thrice) in enumerate(jobs):
                if i >= 2:
                    sp.wait_ge(s_job, i - 1)
                rows = min(MAIN, src.shape[0])
                sp.dma_start(plain[i % 2][0:rows, 0:cols], src[0:rows, :]).then_inc(s_load[i], 16)
                if src.shape[0] == D:
                    for c in range(3):
                        sp.dma_start(plain_rem[i % 2][c * REM:(c + 1) * REM, 0:cols], src[MAIN:D, :]).then_inc(s_load[i], 16)

        @block.scalar
        def _(act):
            if fills:
                act.wait_ge(s_fill, len(fills))
            with nc.allow_non_contiguous_dma(reason="small parameters, one value per partition"):
                for dst, src in extra_loads:
                    act.dma_start(dst, src).then_inc(s_extra, 16)
            act.wait_ge(s_extra, 16 * len(extra_loads))

        @block.gpsimd
        def _(pool):
            for dst in fills:
                nc.gpsimd.memset(dst, 0.0).then_inc(s_fill, 1)

        @block.vector
        def _(dve):
            links = [0]

            def link(instruction):
                links[0] += 1
                instruction.then_inc(s_link, 1)
                dve.wait_ge(s_link, links[0])

            for i, (src, parts, cols, scale, thrice) in enumerate(jobs):
                rows, two = min(MAIN, src.shape[0]), src.shape[0] == D
                dve.wait_ge(s_load[i], 16 * (4 if two else 1))
                high, low, stack = parts
                wide = GROUPS * P if thrice else cols
                for part in range(2 if two else 1):
                    r = STACK if part else rows
                    w = (plain_rem if part else plain)[i % 2][0:r, 0:cols]
                    if thrice:
                        t = (scaled_rem if part else scaled)[0:r, 0:wide]
                        link(nc.vector.memset(t, 0.0))
                        dh = cols // HEADS
                        link(nc.vector.tensor_scalar(
                            t.rearrange("p (h c) -> p h c", h=HEADS)[:, :, 0:3 * dh].rearrange("p h (c d) -> p h c d", c=3),
                            w.rearrange("p (h d) -> p h d", h=HEADS).unsqueeze(2).broadcast_to([r, HEADS, 3, dh]),
                            scale, None, ALU.mult))
                        w = t
                    elif scale != 1.0:
                        t = (scaled_rem if part else scaled)[0:r, 0:wide]
                        link(nc.vector.tensor_scalar(t, w, scale, None, ALU.mult))
                        w = t
                    if part == 0:
                        link(nc.vector.tensor_copy(high[0:r, 0:wide], w))
                        link(nc.vector.tensor_tensor(low[0:r, 0:wide], w, high[0:r, 0:wide].bitcast(F32), ALU.subtract))
                    else:
                        link(nc.vector.tensor_copy(rem_high[0:r, 0:wide], w))
                        link(nc.vector.scalar_tensor_tensor(
                            out=stack[0:r, 0:wide], in0=rem_high[0:r, 0:wide].bitcast(F32), scalar=m.minus_last_row[0:r, 0:1],
                            in1=w, op0=ALU.mult, op1=ALU.add))
                nc.vector.memset(m.scrap[:, i:i + 1], 0.0).then_inc(s_job, 1)


def products(nc, out, pairs):
    for i, (stationary, moving) in enumerate(pairs):
        last = nc.tensor.matmul(out, stationary, moving, start=(i == 0), stop=(i == len(pairs) - 1))
    return last


def norm_loads(m, g, b, out_bias):
    loads = []
    for c, v in ((0, g), (1, b)):
        col = v.rearrange("(n a) -> n a", a=1)
        loads.append((m.norm_cols[:, c:c + 1], col[0:MAIN, :]))
        loads += [(m.norm_cols[r * REM:(r + 1) * REM, c + 2:c + 3], col[MAIN:D, :]) for r in range(4)]
    loads.append((m.out_bias[:], out_bias.rearrange("(a n) -> a n", a=1).broadcast_to([P, D])))
    return loads


def attention(m, tag, dh, cross, g, b, wq, wk, wv, wo, bo, context, x_loads=None):
    nc = m.nc
    small = dh < 32
    NK = CTX_TOK if cross else TOK
    TILES = GROUPS if small else HEADS * dh // P
    inner = HEADS * dh
    scale = float(dh) ** -0.5
    VCH = inner if small else inner // GROUPS
    KD = CTX_D if cross else MAIN

    wo_tiles = m.wo[:, 0:TILES, :]
    loads = norm_loads(m, g, b, bo)
    fills = []
    if small:
        fills.append(wo_tiles)
        for j in range(GROUP):
            loads.append((m.wo[32 * j:32 * j + dh, 0:TILES, :], wo.rearrange("(g j d) n -> j d g n", g=GROUPS, j=GROUP)[j]))
    else:
        loads.append((wo_tiles, wo.rearrange("(t p) n -> p t n", p=P)))
    prepare_weights(m, tag + "w", [(wq, m.wparts[0], inner, scale, small), (wk, m.wparts[1], inner, 1.0, small),
                                   (wv, m.wparts[2], inner, 1.0, False)], loads, fills)

    with ExitStack() as ctx:
        sb = lambda name, shape, dt=F32: ctx.enter_context(nc.sbuf_tensor(f"{tag}_{name}", shape, dt))
        sem = lambda name: m.semaphore(ctx, f"{tag}_{name}")
        bank = lambda name: ctx.enter_context(nc.psum_tensor(f"{tag}_{name}_bank", [P, 512], F32))
        scores_banks = ctx.enter_context(nc.psum_tensor(f"{tag}_scores_banks", [P, 2, 512], F32))
        SCORES_LAG = 1 if small else 0

        def head_scores(k, j):
            bank, col = (k % 2, j * NK) if small else (j % 2, (j // 2) * NK)
            return scores_banks[:, bank, col:col + NK]

        pt_bank, out_bank, qk_bank, v_bank, y_bank, h_bank = (bank(x) for x in ("pt", "out", "qk", "v", "y", "h"))
        s_ctx_high = sem("ctx_high")
        s_ctx_split = sem("ctx_split")
        norm = Norm(m, ctx, tag, h_bank, (lambda n: (s_ctx_split, n)) if cross else (lambda n: (s_ctx_split, 0)))
        if small:
            qstack = [sb(f"qstack{i}", [P, TILES, PAIR * P], F32R) for i in range(2)]
            kstack = sb("kstack", [P, TILES, PAIR * NK], F32R)
            kblocks = [sb(f"kblocks{i}", [P, TILES, PAIR, GROUP * NK], F32R) for i in range(2)]
            qk_high = [sb(f"qk_high{i}", [P, 512], F32R) for i in range(2)]
        else:
            qk = [sb(f"qk{i}", [P, TILES, 512]) for i in range(2)]
        VW = 32 if small else dh
        v = [sb(f"v{i}", [P, HEADS, VW]) for i in range(4)]
        probs = [sb(f"probs{i}", [P, GROUP, NK]) for i in range(4)]
        negmax = [sb(f"negmax{i}", [P, GROUP]) for i in range(4)]
        sums = [sb(f"sums{i}", [P, GROUP]) for i in range(4)]
        rsums = [sb(f"rsums{i}", [P, GROUP]) for i in range(4)]
        probsT = [sb(f"probsT{i}", [P, GROUP, P]) for i in range(2)]
        OT = 1 if small else 2
        outT = [sb(f"outT{i}", [P, OT * P]) for i in range(2)]
        if cross:
            ctx_in = [sb(f"ctx_in{i}", [P, PAIR, CTX_D]) for i in range(2)]
            ctx_high = [sb(f"ctx_high{i}", [P, PAIR * NK], F32R) for i in range(2)]
            ctx_low = [sb(f"ctx_low{i}", [P, PAIR * NK], F32R) for i in range(2)]

        s_x = sem("x_in")
        s_ctx = [sem(f"ctx_in{i}") for i in range(2)]
        s_ctxT = sem("ctxT")
        s_scores = sem("scores")
        s_negmax = sem("negmax_ready")
        s_exp = sem("exp")
        s_rsums = sem("rsums_ready")
        s_probs = sem("probs_ready")
        s_pt = sem("pt")
        s_probsT = sem("probsT_ready")
        s_out = sem("heads_out")
        s_outT = sem("outT_ready")
        s_wo = sem("wo")
        s_resid = sem("resid")
        s_qkproj = sem("qkproj")
        s_qkhigh = sem("qkhigh")
        s_qk = sem("qk_ready")
        s_kblocks = [sem(f"kblocks{i}_ready") for i in range(2)]
        s_vproj = sem("vproj")
        s_v = sem("v_ready")
        s_zero = sem("zeroed")
        zeroed = [t[:] for t in kblocks + v] if small else []
        QKN = TILES // GROUPS * GROUPS
        VN = PAIR if small else PSTEPS
        ctx.callback(m.end_stage)
        block = ctx.enter_context(nc.Block())

        number = lambda q, k: q * QSTEPS + k
        pair_of = lambda q, k: q * 2 + k // PSTEPS
        seq_of = lambda q, k: q * 4 + k // GROUPS

        def tile_at(q, k):
            s = k % PSTEPS
            if not live(pair_of(q, k) + 1, PAIRS) or s >= TILES:
                return None
            return s, (k // PSTEPS + 1) % 2, (pair_of(q, k) + 1) * TILES + s

        def chunk_at(q, k):
            s = k % PSTEPS
            if not live(pair_of(q, k) + 1, PAIRS):
                return None
            if small:
                if s not in (GROUPS, GROUPS + 1):
                    return None
                a, c = s - GROUPS, 0
            else:
                a, c = s // GROUPS, s % GROUPS
            return a, c, (2 * (k // PSTEPS + 1) + a) % 4, (pair_of(q, k) + 1) * VN + (a if small else s)

        def run(engine, step):
            for k in range(-2 * PSTEPS, QSTEPS):
                step(0, k)
            with engine.Fori(1, QUADS - 1) as q:
                for k in range(QSTEPS):
                    step(q, k)
            for k in range(QSTEPS + 5):
                step(QUADS - 1, k)

        @block.sync
        def _(sp):
            for dst, src in x_loads or []:
                sp.dma_start(dst, src).then_inc(s_x, 16)

            def step(q, k):
                n, ahead = number(q, k), pair_of(q, k) + 2
                if cross and k % PSTEPS == 0 and live(ahead, PAIRS):
                    par = (k // PSTEPS) % 2
                    source = context(address(sp, q * 4 + 2 * (k // PSTEPS) + 4))
                    if due(ahead - 1):
                        sp.wait_ge(s_ctxT, ahead - 1)
                    sp.dma_start(ctx_in[par][0:NK, :, :], source).then_inc(s_ctx[par], 16)
                if small and k % PSTEPS == GROUPS and live(ahead - 1, PAIRS):
                    par = (k // PSTEPS + 1) % 2
                    if isinstance(n, int) and n < 0:
                        sp.wait_ge(s_zero, len(zeroed))
                    if due(ahead * TILES):
                        sp.wait_ge(s_qk, ahead * TILES)
                    for j in range(GROUP):
                        rows = slice(32 * j, 32 * j + 32)
                        sp.dma_start(kblocks[par][rows, :, :, j * NK:(j + 1) * NK].bitcast(F32),
                                     kstack[rows, :, :].bitcast(F32).rearrange("p t (a k) -> p t a k", a=PAIR)).then_inc(s_kblocks[par], 16)

            run(sp, step)

        @block.gpsimd
        def _(pool):
            for t in zeroed:
                nc.gpsimd.memset(t.bitcast(F32) if t.dtype == F32R else t, 0.0).then_inc(s_zero, 1)

            def step(q, k):
                n, s, ahead = number(q, k), k % PSTEPS, pair_of(q, k) + 2
                if s == 1 and live(ahead, PAIRS):
                    norm.gpsimd_rstd(pool, ahead)
                if s == 3 and live(ahead, PAIRS):
                    norm.gpsimd_bias(pool, ahead, q * 4 + 2 * (k // PSTEPS) + 4)
                if live(n - 1, STEPS):
                    i = (k - 1) % 4
                    if due(n):
                        pool.wait_ge(s_rsums, n)
                    nc.gpsimd.tensor_tensor(probs[i][:], probs[i][:], rsums[i][:].unsqueeze(2).broadcast_to([P, GROUP, NK]),
                                            ALU.mult).then_inc(s_probs, 1)

            run(pool, step)

        @block.scalar
        def _(act):
            def step(q, k):
                n, s, ahead = number(q, k), k % PSTEPS, pair_of(q, k) + 2
                if live(n, STEPS):
                    i = k % 4
                    if due(n + 1):
                        act.wait_ge(s_negmax, n + 1)
                    if due(n - 3):
                        act.wait_ge(s_pt, n - 3)
                    for j in range(GROUP):
                        last = nc.scalar.activation(probs[i][:, j, :], head_scores(k, j), ACT.Exp,
                                                    bias=negmax[i][:, j:j + 1], scale=1.0, accum_out=sums[i][:, j:j + 1])
                    last.then_inc(s_exp, 1)
                tile = tile_at(q, k)
                if tile:
                    t, par, r = tile
                    width = PAIR * P + PAIR * NK
                    if due(r + 1):
                        act.wait_ge(s_qkproj, r + 1)
                    if small:
                        if due(r - 1):
                            act.wait_ge(s_qk, r - 1)
                        nc.scalar.copy(qk_high[t % 2][:, 0:width], qk_bank[:, 0:width]).then_inc(s_qkhigh, 1)
                    else:
                        if due(n):
                            act.wait_ge(s_scores, n)
                        nc.scalar.copy(qk[par][:, t, 0:width], qk_bank[:, 0:width]).then_inc(s_qk, 1)
                chunk = chunk_at(q, k)
                if chunk:
                    a, c, slot, r = chunk
                    if due(r + 1):
                        act.wait_ge(s_vproj, r + 1)
                    if due((pair_of(q, k) - 1) * PSTEPS + (a + 1) * GROUPS):
                        act.wait_ge(s_out, (pair_of(q, k) - 1) * PSTEPS + (a + 1) * GROUPS)
                    if small:
                        if isinstance(n, int) and n < 0:
                            act.wait_ge(s_zero, len(zeroed))
                        nc.scalar.copy(v[slot][0:NK, :, 0:dh], v_bank[0:NK, 0:inner].rearrange("p (h d) -> p h d", h=HEADS))\
                            .then_inc(s_v, 1)
                    else:
                        nc.scalar.copy(v[slot][0:NK, c * GROUP:(c + 1) * GROUP, :],
                                       v_bank[0:NK, 0:VCH].rearrange("p (h d) -> p h d", h=GROUP)).then_inc(s_v, 1)
                if s == 4 and live(ahead, PAIRS):
                    norm.scalar_affine(act, ahead, (k // PSTEPS) % 2, (s_vproj, (ahead - 1) * VN))
                if cross and s == 6 and live(ahead, PAIRS):
                    par = (k // PSTEPS) % 2
                    if due(ahead + 1):
                        act.wait_ge(s_ctxT, ahead + 1)
                    if due((ahead - 1) * VN):
                        act.wait_ge(s_vproj, (ahead - 1) * VN)
                    nc.scalar.copy(ctx_high[par][0:CTX_D, :], h_bank[0:CTX_D, 0:PAIR * NK]).then_inc(s_ctx_high, 1)

            run(act, step)

        @block.vector
        def _(dve):
            if x_loads:
                dve.wait_ge(s_x, 16 * len(x_loads))

            def step(q, k):
                n, s, ahead = number(q, k), k % PSTEPS, pair_of(q, k) + 2
                seq_ahead = q * 4 + 2 * (k // PSTEPS) + 4
                if s == 1 and live(ahead, PAIRS):
                    norm.wait_stats(dve, ahead)
                if live(n, STEPS):
                    if due(n + 1):
                        dve.wait_ge(s_scores, n + 1)
                    if due(n - 3):
                        dve.wait_ge(s_exp, n - 3)
                    if small:
                        heads, best = scores_banks[:, k % 2, 0:GROUP * NK].rearrange("p (h k) -> p h k", h=GROUP), negmax[k % 4][:]
                    else:
                        heads = scores_banks[:, :, 0:2 * NK].rearrange("p b (c k) -> p b c k", c=2)
                        best = negmax[k % 4][:].rearrange("p (c b) -> p b c", b=2)
                    nc.vector.tensor_reduce(out=best, in_=heads, axis=AX.X, op=ALU.max, negate=True).then_inc(s_negmax, 1)
                if s == 1 and live(ahead, PAIRS):
                    norm.vector_moments(dve, ahead)
                if live(n - 1, STEPS):
                    i = (k - 1) % 4
                    if due(n):
                        dve.wait_ge(s_exp, n)
                    if due(n - 4):
                        dve.wait_ge(s_probs, n - 4)
                    nc.vector.reciprocal(rsums[i][:], sums[i][:]).then_inc(s_rsums, 1)
                if live(n - 2, STEPS):
                    i = k % 2
                    if due(n - 1):
                        dve.wait_ge(s_pt, n - 1)
                    if due(n - 3):
                        dve.wait_ge(s_out, n - 3)
                    nc.vector.tensor_copy(probsT[i][0:NK, :, :], pt_bank[0:NK, :].rearrange("p (h k) -> p h k", h=GROUP))\
                        .then_inc(s_probsT, 1)
                tile = tile_at(q, k)
                if tile and small:
                    t, par, r = tile
                    if due(r + 1):
                        dve.wait_ge(s_qkhigh, r + 1)
                    if s == 0:
                        if due(16 * GROUP * half(q, k)):
                            dve.wait_ge(s_kblocks[(par + 1) % 2], 16 * GROUP * half(q, k))
                    high = qk_high[t % 2][:].bitcast(F32)
                    width = PAIR * P
                    nc.vector.scalar_tensor_tensor(out=qstack[par][:, t, :], in0=high[:, 0:width], scalar=m.minus_low8[:, 0:1],
                                                   in1=qk_bank[:, 0:width], op0=ALU.mult, op1=ALU.add)
                    nc.vector.scalar_tensor_tensor(out=kstack[:, t, :], in0=high[:, width:width + PAIR * NK],
                                                   scalar=m.minus_last8[:, 0:1], in1=qk_bank[:, width:width + PAIR * NK],
                                                   op0=ALU.mult, op1=ALU.add).then_inc(s_qk, 1)
                if live(n - 3, STEPS):
                    i = (k - 3) % 2
                    if due(n - 2):
                        dve.wait_ge(s_out, n - 2)
                    if due(n - 4):
                        dve.wait_ge(s_wo, n - 4)
                    nc.vector.tensor_copy(outT[i][:], out_bank[:, 0:OT * P]).then_inc(s_outT, 1)
                if live(n - 4, STEPS) and (k - 4) % GROUPS == GROUPS - 1:
                    seq = seq_of(q, k - 4)
                    if due(n - 3):
                        dve.wait_ge(s_wo, n - 3)
                    if due(pair_of(q, k - 4) + 1):
                        dve.wait_ge(norm.s_biased, pair_of(q, k - 4) + 1)
                    xt = m.x1(seq)
                    nc.vector.tensor_tensor(xt, y_bank[:, 0:D], xt, ALU.add).then_inc(s_resid, 1)
                if s == 0 and live(ahead, PAIRS):
                    norm.vector_stats(dve, ahead, seq_ahead)
                if s == 2 and live(ahead, PAIRS):
                    norm.vector_h(dve, ahead, seq_ahead)
                if s == 5 and live(ahead, PAIRS):
                    norm.vector_split(dve, ahead, (k // PSTEPS) % 2)
                if cross and s == 7 and live(ahead, PAIRS):
                    par = (k // PSTEPS) % 2
                    if due(ahead + 1):
                        dve.wait_ge(s_ctx_high, ahead + 1)
                    nc.vector.tensor_tensor(ctx_low[par][0:CTX_D, :], h_bank[0:CTX_D, 0:PAIR * NK],
                                            ctx_high[par][0:CTX_D, :].bitcast(F32), ALU.subtract).then_inc(s_ctx_split, 1)

            def half(q, k):
                return q + (k // PSTEPS + 1) // 2 if (k // PSTEPS + 1) % 2 == 0 else q + (k // PSTEPS + 1 + 1) // 2

            run(dve, step)

        @block.tensor
        def _(pe):
            def step(q, k):
                n, s, ahead = number(q, k), k % PSTEPS, pair_of(q, k) + 2
                a, grp = (k % PSTEPS) // GROUPS, k % GROUPS
                par = (k // PSTEPS) % 2
                if live(n, STEPS):
                    if due(n - SCORES_LAG):
                        pe.wait_ge(s_exp, n - SCORES_LAG)
                    if s == 0:
                        if small:
                            pe.wait_ge(s_kblocks[par], (q + 1) * (16 * GROUP))
                        pe.wait_ge(s_qk, (pair_of(q, k) + 1) * TILES)
                    if small:
                        last = nc.tensor.matmul(scores_banks[:, k % 2, 0:GROUP * NK], qstack[par][:, grp, a * P:(a + 1) * P],
                                                kblocks[par][:, grp, a, :], start=True, stop=True)
                    else:
                        for j in range(GROUP):
                            rows, t = slice(dh * (j % 2), dh * (j % 2) + dh), 2 * grp + j // 2
                            last = nc.tensor.matmul(head_scores(k, j), qk[par][rows, t, a * P:(a + 1) * P],
                                                    qk[par][rows, t, PAIR * P + a * NK:PAIR * P + (a + 1) * NK], start=True, stop=True)
                    last.then_inc(s_scores, 1)
                tile = tile_at(q, k)
                if tile:
                    t, tpar, r = tile
                    if s == 0:
                        if due(ahead):
                            pe.wait_ge(norm.s_split, ahead)
                        if cross:
                            if due(ahead):
                                pe.wait_ge(s_ctx_split, ahead)
                    if due(r):
                        pe.wait_ge(s_qk, r)
                    cols = slice(t * P, (t + 1) * P)
                    (qh, ql, qs), (kh, kl, ks) = m.wparts[0], m.wparts[1]
                    hh, hl, hs = norm.high[tpar][:], norm.low[tpar][:], norm.stack[tpar][0:STACK, :]
                    products(nc, qk_bank[:, 0:PAIR * P],
                             [(qh[:, cols], hh), (qh[:, cols], hl), (ql[:, cols], hh), (qs[0:STACK, cols], hs)])
                    kout = qk_bank[:, PAIR * P:PAIR * P + PAIR * NK]
                    if cross:
                        ch, cl = ctx_high[tpar][0:CTX_D, :], ctx_low[tpar][0:CTX_D, :]
                        last = products(nc, kout, [(kh[0:CTX_D, cols], ch), (kh[0:CTX_D, cols], cl), (kl[0:CTX_D, cols], ch)])
                    else:
                        last = products(nc, kout, [(kh[:, cols], hh), (kh[:, cols], hl), (kl[:, cols], hh), (ks[0:STACK, cols], hs)])
                    last.then_inc(s_qkproj, 1)
                if live(n - 2, STEPS):
                    if due(n - 1):
                        pe.wait_ge(s_probs, n - 1)
                    if due(n - 2):
                        pe.wait_ge(s_probsT, n - 2)
                    for j in range(GROUP):
                        last = nc.tensor.transpose(pt_bank[0:NK, j * P:(j + 1) * P], probs[(k - 2) % 4][:, j, :], m.ident[:])
                    last.then_inc(s_pt, 1)
                chunk = chunk_at(q, k)
                if chunk:
                    ca, c, slot, r = chunk
                    tpar = (k // PSTEPS + 1) % 2
                    if due(r):
                        pe.wait_ge(s_v, r)
                    cols = slice(c * VCH, (c + 1) * VCH)
                    vh, vl, vs = m.wparts[2]
                    if cross:
                        tok = slice(ca * NK, (ca + 1) * NK)
                        ch, cl = ctx_high[tpar][0:CTX_D, tok], ctx_low[tpar][0:CTX_D, tok]
                        last = products(nc, v_bank[0:NK, 0:VCH],
                                        [(ch, vh[0:CTX_D, cols]), (ch, vl[0:CTX_D, cols]), (cl, vh[0:CTX_D, cols])])
                    else:
                        tok = slice(ca * P, (ca + 1) * P)
                        hh, hl, hs = norm.high[tpar][:, tok], norm.low[tpar][:, tok], norm.stack[tpar][0:STACK, tok]
                        last = products(nc, v_bank[:, 0:VCH],
                                        [(hh, vh[:, cols]), (hh, vl[:, cols]), (hl, vh[:, cols]), (hs, vs[0:STACK, cols])])
                    last.then_inc(s_vproj, 1)
                if live(n - 3, STEPS):
                    if due(n - 2):
                        pe.wait_ge(s_probsT, n - 2)
                    if due(n - 3):
                        pe.wait_ge(s_outT, n - 3)
                    g3, slot = (k - 3) % GROUPS, ((k - 3) // GROUPS) % 4
                    if g3 == 0:
                        if small:
                            pe.wait_ge(s_v, seq_of(q, k - 3) + 1)
                        else:
                            pe.wait_ge(s_v, (seq_of(q, k - 3) + 1) * GROUPS)
                    for j in range(GROUP):
                        rows, col = (32 * j, 0) if small else (dh * (j % 2), j // 2)
                        last = nc.tensor.matmul(out_bank[rows:rows + VW, col * P:(col + 1) * P], v[slot][0:NK, g3 * GROUP + j, :],
                                                probsT[(k - 3) % 2][0:NK, j, :], start=True, stop=True)
                    last.then_inc(s_out, 1)
                if live(n - 4, STEPS):
                    g4 = (k - 4) % GROUPS
                    if due(n - 3):
                        pe.wait_ge(s_outT, n - 3)
                    if g4 == 0:
                        if due(seq_of(q, k - 4)):
                            pe.wait_ge(s_resid, seq_of(q, k - 4))
                    for t in range(OT):
                        last = nc.tensor.matmul(y_bank[:, 0:D], outT[(k - 4) % 2][:, t * P:(t + 1) * P], m.wo[:, g4 * OT + t, :],
                                                start=(g4 == 0 and t == 0), stop=(g4 == GROUPS - 1 and t == OT - 1))
                    last.then_inc(s_wo, 1)
                if s == 4 and live(ahead, PAIRS):
                    norm.tensor_transpose(pe, ahead)
                if cross and s == 6 and live(ahead, PAIRS):
                    cpar = (k // PSTEPS) % 2
                    if due(ahead * 2 + 2):
                        pe.wait_ge(norm.s_y, ahead * 2 + 2)
                    pe.wait_ge(s_ctx[cpar], (q + (k // PSTEPS + 2) // 2 + 1) * 16 if cpar == 0 else (q + (k // PSTEPS + 1) // 2 + 1) * 16)
                    for b2 in range(PAIR):
                        last = nc.tensor.transpose(h_bank[0:CTX_D, b2 * NK:(b2 + 1) * NK], ctx_in[cpar][0:NK, b2, :], m.ident[0:NK, 0:NK])
                    last.then_inc(s_ctxT, 1)

            run(pe, step)


def feed_forward(m, tag, gelu, g, b, w1, b1, w2, b2, out=None):
    nc = m.nc
    TILES = FF // P
    bias1 = m.bias1
    loads = norm_loads(m, g, b, b2)
    loads.append((bias1[:], b1.rearrange("(t p) -> p t", p=P)))
    loads.append((m.wo[:, 0:TILES, :], w2.rearrange("(t p) n -> p t n", p=P)))
    prepare_weights(m, tag + "w", [(w1, m.wparts[0], 2 * FF, 1.0, False)], loads)
    with ExitStack() as ctx:
        sb = lambda name, shape, dt=F32: ctx.enter_context(nc.sbuf_tensor(f"{tag}_{name}", shape, dt))
        sem = lambda name: m.semaphore(ctx, f"{tag}_{name}")
        bank = lambda name: ctx.enter_context(nc.psum_tensor(f"{tag}_{name}_bank", [P, 512], F32))
        up_bank = [bank(f"up{i}") for i in range(2)]
        y_bank = [[bank(f"y{i}{a}") for a in range(PAIR)] for i in range(2)]
        h_bank = bank("h")
        s_never = sem("unused")
        norm = Norm(m, ctx, tag, h_bank, lambda n: (s_never, 0))
        gate = [sb(f"gate{i}", [P, PAIR * P]) for i in range(2)]
        act_t = [sb(f"hidden{i}", [P, PAIR * P]) for i in range(2)]
        s_up = sem("up")
        s_gate = sem("gate_ready")
        s_hidden = sem("hidden_ready")
        s_down = sem("down")
        s_resid = sem("resid")
        s_store = sem("store")
        ctx.callback(m.end_stage)
        block = ctx.enter_context(nc.Block())
        BODY = 2 * TILES
        number = lambda q, k: q * BODY + k
        pair_of = lambda q, k: q * 2 + k // TILES
        TOTAL = PAIRS * TILES

        def run(engine, step):
            for k in range(-TILES, BODY):
                step(0, k)
            with engine.Fori(1, QUADS - 1) as q:
                for k in range(BODY):
                    step(q, k)
            for k in range(BODY + 4):
                step(QUADS - 1, k)

        @block.sync
        def _(sp):
            if out is None:
                return

            def step(q, k):
                n = number(q, k)
                if (k - 3) % TILES == TILES - 1 and live(n - 3, TOTAL):
                    seq = address(sp, q * 4 + 2 * ((k - 3) // TILES))
                    if due(pair_of(q, k - 3) + 1):
                        sp.wait_ge(s_resid, pair_of(q, k - 3) + 1)
                    sp.dma_start(out[bass.ds(seq, PAIR), :, :].rearrange("s p d -> p s d"), m.xpair(seq)).then_inc(s_store, 16)

            run(sp, step)
            sp.wait_ge(s_store, 16 * PAIRS)

        @block.gpsimd
        def _(pool):
            def step(q, k):
                s, ahead = k % TILES, pair_of(q, k) + 1
                if live(ahead, PAIRS):
                    if s == 1:
                        norm.gpsimd_rstd(pool, ahead)
                    if s == 2:
                        norm.gpsimd_bias(pool, ahead, q * 4 + 2 * (k // TILES) + 2)

            run(pool, step)

        @block.scalar
        def _(act):
            def step(q, k):
                n, s, ahead = number(q, k), k % TILES, pair_of(q, k) + 1
                if live(n, TOTAL):
                    if due(n + 1):
                        act.wait_ge(s_up, n + 1)
                    if due(n - 1):
                        act.wait_ge(s_hidden, n - 1)
                    nc.scalar.activation(gate[k % 2][:], up_bank[k % 2][:, PAIR * P:], gelu,
                                         bias=bias1[:, TILES + s:TILES + s + 1], scale=1.0).then_inc(s_gate, 1)
                if s == 2 and live(ahead, PAIRS):
                    norm.scalar_affine(act, ahead, (k // TILES + 1) % 2, (s_up, (ahead - 1) * TILES))

            run(act, step)

        @block.vector
        def _(dve):
            def step(q, k):
                n, s, ahead = number(q, k), k % TILES, pair_of(q, k) + 1
                seq_ahead = q * 4 + 2 * (k // TILES) + 2
                if s == 1 and live(ahead, PAIRS):
                    norm.wait_stats(dve, ahead)
                if live(n, TOTAL):
                    if due(n + 1):
                        dve.wait_ge(s_gate, n + 1)
                    if due(n - 1):
                        dve.wait_ge(s_down, n - 1)
                    nc.vector.scalar_tensor_tensor(out=act_t[k % 2][:], in0=up_bank[k % 2][:, 0:PAIR * P],
                                                   scalar=bias1[:, s:s + 1], in1=gate[k % 2][:], op0=ALU.add,
                                                   op1=ALU.mult).then_inc(s_hidden, 1)
                if (k - 3) % TILES == TILES - 1 and live(n - 3, TOTAL):
                    seq, ypar = q * 4 + 2 * ((k - 3) // TILES), ((k - 3) // TILES) % 2
                    if due(n - 2):
                        dve.wait_ge(s_down, n - 2)
                    if due(pair_of(q, k - 3) + 1):
                        dve.wait_ge(norm.s_biased, pair_of(q, k - 3) + 1)
                    for a in range(PAIR):
                        xt = m.xs(seq, a)
                        last = nc.vector.tensor_tensor(xt, y_bank[ypar][a][:, 0:D], xt, ALU.add)
                    last.then_inc(s_resid, 1)
                if live(ahead, PAIRS):
                    if s == 0:
                        norm.vector_stats(dve, ahead, seq_ahead)
                    if s == 1:
                        norm.vector_moments(dve, ahead)
                        norm.vector_h(dve, ahead, seq_ahead)
                    if s == 3:
                        norm.vector_split(dve, ahead, (k // TILES + 1) % 2)

            run(dve, step)

        @block.tensor
        def _(pe):
            def step(q, k):
                n, s, ahead = number(q, k), k % TILES, pair_of(q, k) + 1
                par = (k // TILES) % 2
                if live(n, TOTAL):
                    if s == 0:
                        pe.wait_ge(norm.s_split, pair_of(q, k) + 1)
                    if due(n - 1):
                        pe.wait_ge(s_hidden, n - 1)
                    wh, wl, ws = m.wparts[0]
                    hh, hl, hs = norm.high[par][:], norm.low[par][:], norm.stack[par][0:STACK, :]
                    for half in range(2):
                        cols = slice(half * FF + s * P, half * FF + (s + 1) * P)
                        last = products(nc, up_bank[k % 2][:, half * PAIR * P:(half + 1) * PAIR * P],
                                        [(wh[:, cols], hh), (wh[:, cols], hl), (wl[:, cols], hh), (ws[0:STACK, cols], hs)])
                    last.then_inc(s_up, 1)
                if live(n - 2, TOTAL):
                    t, ypar = (k - 2) % TILES, ((k - 2) // TILES) % 2
                    if due(n - 1):
                        pe.wait_ge(s_hidden, n - 1)
                    if t == 0:
                        if due(pair_of(q, k - 2) - 1):
                            pe.wait_ge(s_resid, pair_of(q, k - 2) - 1)
                    for a in range(PAIR):
                        last = nc.tensor.matmul(y_bank[ypar][a][:, 0:D], act_t[k % 2][:, a * P:(a + 1) * P], m.wo[:, t, :],
                                                start=(t == 0), stop=(t == TILES - 1))
                    last.then_inc(s_down, 1)
                if s == 2 and live(ahead, PAIRS):
                    norm.tensor_transpose(pe, ahead)

            run(pe, step)


def build(nc, A, out):
    m = Machine(nc)
    with ExitStack() as ctx:
        sb = lambda name, shape, dt=F32: ctx.enter_context(nc.sbuf_tensor(name, shape, dt))
        m.x = sb("x_tokens", [P, SEQS * D])
        m.wparts = [[sb(f"w{i}_{part}", [P, 1280], F32R) for part in ("high", "low", "stack")] for i in range(3)]
        m.wo = sb("w_out", [P, 10, D])
        m.norm_cols = sb("norm_cols", [P, 4])
        m.out_bias = sb("out_bias", [P, D])
        m.bias1 = sb("bias1", [P, 2 * FF // P])
        m.ident = sb("ident", [P, P])
        m.eps = sb("eps", [P, PAIR])
        m.minus_half = sb("minus_half", [P, PAIR])
        m.minus_low_row = sb("minus_low_row", [P, 1])
        m.minus_last_row = sb("minus_last_row", [P, 1])
        m.minus_low8 = sb("minus_low8", [P, 1])
        m.minus_last8 = sb("minus_last8", [P, 1])
        m.scrap = sb("scrap", [P, 4])
        band = sb("band", [P, 2, GROUP])
        m.x1 = lambda seq: m.x[:, bass.ds(seq * D, D)]
        m.xs = lambda seq, a: m.x[:, bass.ds(seq * D + a * D, D)]
        m.xpair = lambda seq: m.x[:, bass.ds(seq * D, PAIR * D)].rearrange("p (a d) -> p a d", a=PAIR)

        with ExitStack() as c0:
            s_pool = m.semaphore(c0, "const_pool")
            c0.callback(m.end_stage)
            block = c0.enter_context(nc.Block())

            @block.gpsimd
            def _(pool):
                made = [0]

                def link(instruction):
                    made[0] += 1
                    instruction.then_inc(s_pool, 1)
                    pool.wait_ge(s_pool, made[0])

                link(nc.gpsimd.memset(m.ident[:], 0.0))
                link(nc.gpsimd.affine_select(out=m.ident[:], in_=m.ident[:], compare_op=ALU.not_equal, fill=1.0, base=0,
                                             pattern=[[-1, P]], channel_multiplier=1))
                link(nc.gpsimd.memset(m.minus_half[:], -0.5))
                link(nc.gpsimd.memset(m.eps[:], EPS))
                for tile, row in ((m.minus_low_row, 1), (m.minus_last_row, 2)):
                    link(nc.gpsimd.memset(tile[:], 0.0))
                    link(nc.gpsimd.memset(tile[row * REM:(row + 1) * REM, :], -1.0))
                link(nc.gpsimd.memset(band[:], -1.0))
                for i in range(2):
                    lo = 8 * (i + 1)
                    link(nc.gpsimd.affine_select(out=band[:, i, :], in_=band[:, i, :], compare_op=ALU.is_ge, fill=0.0, base=-lo,
                                                 pattern=[[-32, GROUP]], channel_multiplier=1))
                    link(nc.gpsimd.affine_select(out=band[:, i, :], in_=band[:, i, :], compare_op=ALU.is_ge, fill=0.0,
                                                 base=lo + 7, pattern=[[32, GROUP]], channel_multiplier=-1))

            @block.vector
            def _(dve):
                dve.wait_ge(s_pool, 13)
                for i, tile in enumerate((m.minus_low8, m.minus_last8)):
                    nc.vector.tensor_reduce(out=tile[:], in_=band[:, i, :], axis=AX.X, op=ALU.add)

        x_in, c_in = A["x"], A["ctx_768"]
        context = lambda seq: c_in[bass.ds(seq, PAIR), :, :].rearrange("s p d -> p s d")
        CH = 4
        x_loads = [(m.x[:, i * CH * D:(i + 1) * CH * D].rearrange("p (s d) -> p s d", d=D),
                    x_in[i * CH:(i + 1) * CH, :, :].rearrange("s p d -> p s d")) for i in range(SEQS // CH)]
        L = lambda name: A["L0_xattn_" + name]
        attention(m, "a0", 8, False, L("n1_g"), L("n1_b"), L("q1"), L("k1"), L("v1"), L("o1_w"), L("o1_b"), context, x_loads)
        attention(m, "c0", 8, True, L("n2_g"), L("n2_b"), L("q2"), L("k2"), L("v2"), L("o2_w"), L("o2_b"), context)
        feed_forward(m, "f0", ACT.Gelu, L("n3_g"), L("n3_b"), L("ff_w1"), L("ff_b1"), L("ff_w2"), L("ff_b2"))
        L = lambda name: A["L1_xattn_" + name]
        attention(m, "a1", 64, False, L("g1"), L("be1"), L("wq1"), L("wk1"), L("wv1"), L("wo1"), L("bo1"), context)
        attention(m, "c1", 64, True, L("g2"), L("be2"), L("wq2"), L("wk2"), L("wv2"), L("wo2"), L("bo2"), context)
        feed_forward(m, "f1", ACT.Gelu_apprx_tanh, L("g3"), L("be3"), L("w_ff1"), L("b_ff1"), L("w_ff2"), L("b_ff2"), out)


def kernel(**inputs):
    import concourse.bacc as bacc
    from concourse.bass_utils import run_bass_kernel_spmd

    nc = bacc.Bacc("TRN2", target_bir_lowering=False, num_devices=1)
    arrays, A = {}, {}
    for name, value in inputs.items():
        a = np.ascontiguousarray(value)
        arrays[f"in_{name}"] = a
        A[name] = nc.dram_tensor(f"in_{name}", a.shape, mybir.dt.from_np(a.dtype), kind="ExternalInput").ap()
    out = nc.dram_tensor("out_x", (SEQS, TOK, D), F32, kind="ExternalOutput").ap()
    build(nc, A, out)
    result = run_bass_kernel_spmd(nc, [arrays], core_ids=[0])
    return result.results[0]["out_x"]
```

```python
import numpy as np
import concourse.bass as bass
from concourse import mybir
from contextlib import ExitStack

F32 = mybir.dt.float32
F32R = mybir.dt.float32r
ALU = mybir.AluOpType
ACT = mybir.ActivationFunctionType
AX = mybir.AxisListType

P = 128
SEQS, TOK, D = 64, 128, 160
CTX_TOK, CTX_D = 77, 96
HEADS = 20
FF = 640
MAIN = 128
REM = D - MAIN
STACK = 3 * REM
GROUP = 4
GROUPS = HEADS // GROUP
PAIR = 2
PSTEPS = PAIR * GROUPS
QSTEPS = 2 * PSTEPS
PAIRS = SEQS // PAIR
QUADS = SEQS // (2 * PAIR)
STEPS = SEQS * GROUPS
EPS = 1e-5


def live(value, total):
    return not isinstance(value, int) or 0 <= value < total


def due(count):
    return not isinstance(count, int) or count > 0


def address(engine, value):
    return value if isinstance(value, int) else engine.snap(value)


def clear(nc, semaphores):
    with nc.Block() as block:
        @block.sync
        def _(sp):
            for semaphore in semaphores:
                sp.sem_clear(semaphore)


class Machine:

    def __init__(self, nc):
        self.nc, self.stage_semaphores = nc, []

    def semaphore(self, ctx, name):
        self.stage_semaphores.append(ctx.enter_context(self.nc.semaphore(name)))
        return self.stage_semaphores[-1]

    def end_stage(self):
        clear(self.nc, self.stage_semaphores)
        self.stage_semaphores = []


class Norm:

    def __init__(self, m, ctx, tag, bank, done_reading):
        nc = m.nc
        sb = lambda name, shape, dt=F32: ctx.enter_context(nc.sbuf_tensor(f"{tag}_{name}", shape, dt))
        sem = lambda name: m.semaphore(ctx, f"{tag}_{name}")
        self.m, self.bank, self.done_reading = m, bank, done_reading
        self.stats = sb("stats", [P, PAIR, 6])
        self.moments = sb("moments", [P, PAIR, 2])
        self.var_eps = sb("var_eps", [P, PAIR])
        self.rstd = sb("rstd", [P, PAIR])
        self.h = sb("h", [P, PAIR, 2 * P])
        self.y = sb("y", [P, 2, PAIR * P])
        self.yhigh = sb("yhigh", [P, PAIR * P], F32R)
        self.high = [sb(f"high{i}", [P, PAIR * P], F32R) for i in range(2)]
        self.low = [sb(f"low{i}", [P, PAIR * P], F32R) for i in range(2)]
        self.stack = [sb(f"stack{i}", [P, PAIR * P], F32R) for i in range(2)]
        self.s_stats6 = sem("stats6")
        self.s_moments = sem("moments_ready")
        self.s_vareps = sem("var_eps_ready")
        self.s_rstd = sem("rstd_ready")
        self.s_h = sem("h_ready")
        self.s_biased = sem("x_biased")
        self.s_hT = sem("hT_ready")
        self.s_y = sem("y_ready")
        self.s_high = sem("high_ready")
        self.s_split = sem("split_ready")

    def vector_stats(self, e, n, seq):
        nc, m = self.m.nc, self.m
        if due(n):
            e.wait_ge(self.s_h, n)
        for a in range(PAIR):
            nc.vector.bn_stats(self.stats[:, a, :], m.xs(seq, a)).then_inc(self.s_stats6, 1)

    def wait_stats(self, e, n):
        if due(n * PAIR + PAIR):
            e.wait_ge(self.s_stats6, n * PAIR + PAIR)

    def vector_moments(self, e, n):
        for a in range(PAIR):
            self.m.nc.vector.bn_aggr(self.moments[:, a, :], self.stats[:, a, :]).then_inc(self.s_moments, 1)

    def gpsimd_rstd(self, e, n):
        nc = self.m.nc
        if due(n * PAIR + PAIR):
            e.wait_ge(self.s_moments, n * PAIR + PAIR)
        nc.gpsimd.tensor_tensor(self.var_eps[:], self.moments[:, :, 1], self.m.eps[:], ALU.add).then_inc(self.s_vareps, 1)
        if due(n + 1):
            e.wait_ge(self.s_vareps, n + 1)
        nc.gpsimd.tensor_tensor(self.rstd[:], self.var_eps[:], self.m.minus_half[:], ALU.pow).then_inc(self.s_rstd, 1)

    def vector_h(self, e, n, seq):
        nc, m = self.m.nc, self.m
        if due(n + 1):
            e.wait_ge(self.s_rstd, n + 1)
        if due(n):
            e.wait_ge(self.s_hT, n)
        for a in range(PAIR):
            mean, rstd = self.moments[:, a, 0:1], self.rstd[:, a:a + 1]
            nc.vector.tensor_scalar(self.h[:, a, 0:MAIN], m.xs(seq, a)[:, 0:MAIN], mean, rstd, ALU.subtract, ALU.mult)
            last = nc.vector.tensor_scalar(
                self.h[:, a, MAIN:].rearrange("p (c d) -> p c d", d=REM),
                m.xs(seq, a)[:, MAIN:D].unsqueeze(1).broadcast_to([P, 4, REM]), mean, rstd, ALU.subtract, ALU.mult)
        last.then_inc(self.s_h, 1)

    def gpsimd_bias(self, e, n, seq):
        nc, m = self.m.nc, self.m
        if due(n + 1):
            e.wait_ge(self.s_h, n + 1)
        nc.gpsimd.tensor_tensor(m.xpair(seq), m.xpair(seq), m.out_bias[:].unsqueeze(1).broadcast_to([P, PAIR, D]),
                                ALU.add).then_inc(self.s_biased, 1)

    def tensor_transpose(self, e, n):
        nc = self.m.nc
        if due(n + 1):
            e.wait_ge(self.s_h, n + 1)
        if due(n * 2):
            e.wait_ge(self.s_y, n * 2)
        used, count = self.done_reading(n)
        if due(count):
            e.wait_ge(used, count)
        for part in range(2):
            for a in range(PAIR):
                last = nc.tensor.transpose(self.bank[:, part * PAIR * P + a * P: part * PAIR * P + (a + 1) * P],
                                           self.h[:, a, part * P:(part + 1) * P], self.m.ident[:])
        last.then_inc(self.s_hT, 1)

    def scalar_affine(self, e, n, par, parts_used):
        nc, m = self.m.nc, self.m
        if due(n + 1):
            e.wait_ge(self.s_hT, n + 1)
        if due(n):
            e.wait_ge(self.s_split, n)
        for part in range(2):
            nc.scalar.activation(self.y[:, part, :], self.bank[:, part * PAIR * P:(part + 1) * PAIR * P], ACT.Identity,
                                 bias=m.norm_cols[:, 2 * part + 1:2 * part + 2],
                                 scale=m.norm_cols[:, 2 * part:2 * part + 1]).then_inc(self.s_y, 1)
        if due(n * 2 + 2):
            e.wait_ge(self.s_y, n * 2 + 2)
        used, count = parts_used
        if due(count):
            e.wait_ge(used, count)
        nc.scalar.copy(self.high[par][:], self.y[:, 0, :]).then_inc(self.s_high, 1)
        nc.scalar.copy(self.yhigh[:], self.y[:, 1, :]).then_inc(self.s_high, 1)

    def vector_split(self, e, n, par):
        nc, m = self.m.nc, self.m
        if due(n * 2 + 2):
            e.wait_ge(self.s_high, n * 2 + 2)
        nc.vector.tensor_tensor(self.low[par][:], self.y[:, 0, :], self.high[par][:].bitcast(F32), ALU.subtract)
        nc.vector.scalar_tensor_tensor(out=self.stack[par][:], in0=self.yhigh[:].bitcast(F32), scalar=m.minus_low_row[:, 0:1],
                                       in1=self.y[:, 1, :], op0=ALU.mult, op1=ALU.add).then_inc(self.s_split, 1)


def prepare_weights(m, tag, jobs, extra_loads, fills=(), x_loads=()):
    nc = m.nc
    with ExitStack() as ctx:
        sb = lambda name, shape, dt=F32: ctx.enter_context(nc.sbuf_tensor(f"{tag}_{name}", shape, dt))
        sem = lambda name: m.semaphore(ctx, f"{tag}_{name}")
        WIDE = 1280
        plain = [[sb(f"plain{i}{part}", [P, WIDE]) for part in range(2)] for i in range(len(jobs))]
        scaled = [sb(f"scaled{part}", [P, WIDE]) for part in range(2)]
        rem_high = sb("rem_high", [P, WIDE], F32R)
        s_load = [sem(f"load{i}") for i in range(len(jobs))]
        s_extra = sem("extra")
        s_x = sem("x_in")
        s_scaled = sem("scaled")
        s_high = sem("high")
        s_rest = sem("rest")
        s_zero = sem("zero")
        s_fill = sem("fill")
        ctx.callback(m.end_stage)
        block = ctx.enter_context(nc.Block())

        units = []
        for i, (src, parts, cols, scale, thrice) in enumerate(jobs):
            for part in range(2 if src.shape[0] == D else 1):
                units.append((i, part, STACK if part else min(MAIN, src.shape[0]), thrice or scale != 1.0))

        @block.sync
        def _(sp):
            for i, (src, parts, cols, scale, thrice) in enumerate(jobs):
                rows = min(MAIN, src.shape[0])
                sp.dma_start(plain[i][0][0:rows, 0:cols], src[0:rows, :]).then_inc(s_load[i], 16)
                if src.shape[0] == D:
                    for c in range(3):
                        sp.dma_start(plain[i][1][c * REM:(c + 1) * REM, 0:cols], src[MAIN:D, :]).then_inc(s_load[i], 16)
            for dst, src in x_loads:
                sp.dma_start(dst, src).then_inc(s_x, 16)
            if x_loads:
                sp.wait_ge(s_x, 16 * len(x_loads))

        @block.gpsimd
        def _(pool):
            for dst in fills:
                nc.gpsimd.memset(dst, 0.0).then_inc(s_fill, 1)

        @block.scalar
        def _(act):
            if fills:
                act.wait_ge(s_fill, len(fills))
            with nc.allow_non_contiguous_dma(reason="small parameters, one value per partition"):
                for dst, src in extra_loads:
                    act.dma_start(dst, src).then_inc(s_extra, 16)
            laid = rems = 0
            for u, (i, part, rows, first) in enumerate(units):
                src, (high, low, stack), cols, scale, thrice = jobs[i]
                wide = GROUPS * P if thrice else cols
                w = (scaled[part] if first else plain[i][part])[0:rows, 0:wide]
                laid += first
                if first:
                    act.wait_ge(s_scaled, laid)
                else:
                    act.wait_ge(s_load[i], 16 * (4 if src.shape[0] == D else 1))
                if part and rems:
                    act.wait_ge(s_rest, u - 1)
                rems += part
                nc.scalar.copy((rem_high if part else high)[0:rows, 0:wide], w).then_inc(s_high, 1)
            act.wait_ge(s_extra, 16 * len(extra_loads))

        @block.vector
        def _(dve):
            zeros = 0
            for u, (i, part, rows, first) in enumerate(units):
                src, (high, low, stack), cols, scale, thrice = jobs[i]
                wide = GROUPS * P if thrice else cols
                w = plain[i][part][0:rows, 0:cols]
                dve.wait_ge(s_load[i], 16 * (4 if src.shape[0] == D else 1))
                if first and u >= 2:
                    dve.wait_ge(s_rest, u - 1)
                if thrice:
                    t, dh = scaled[part][0:rows, 0:wide], cols // HEADS
                    nc.vector.memset(t, 0.0).then_inc(s_zero, 1)
                    zeros += 1
                    dve.wait_ge(s_zero, zeros)
                    nc.vector.tensor_scalar(
                        t.rearrange("p (h c) -> p h c", h=HEADS)[:, :, 0:3 * dh].rearrange("p h (c d) -> p h c d", c=3),
                        w.rearrange("p (h d) -> p h d", h=HEADS).unsqueeze(2).broadcast_to([rows, HEADS, 3, dh]),
                        scale, None, ALU.mult).then_inc(s_scaled, 1)
                    w = t
                elif first:
                    nc.vector.tensor_scalar(scaled[part][0:rows, 0:wide], w, scale, None, ALU.mult).then_inc(s_scaled, 1)
                    w = scaled[part][0:rows, 0:wide]
                dve.wait_ge(s_high, u + 1)
                if part:
                    nc.vector.scalar_tensor_tensor(
                        out=stack[0:rows, 0:wide], in0=rem_high[0:rows, 0:wide].bitcast(F32),
                        scalar=m.minus_last_row[0:rows, 0:1], in1=w, op0=ALU.mult, op1=ALU.add).then_inc(s_rest, 1)
                else:
                    nc.vector.tensor_tensor(low[0:rows, 0:wide], w, high[0:rows, 0:wide].bitcast(F32),
                                            ALU.subtract).then_inc(s_rest, 1)


def products(nc, out, pairs):
    for i, (stationary, moving) in enumerate(pairs):
        last = nc.tensor.matmul(out, stationary, moving, start=(i == 0), stop=(i == len(pairs) - 1))
    return last


def norm_loads(m, g, b, out_bias):
    loads = []
    for c, v in ((0, g), (1, b)):
        col = v.rearrange("(n a) -> n a", a=1)
        loads.append((m.norm_cols[:, c:c + 1], col[0:MAIN, :]))
        loads += [(m.norm_cols[r * REM:(r + 1) * REM, c + 2:c + 3], col[MAIN:D, :]) for r in range(4)]
    loads.append((m.out_bias[:], out_bias.rearrange("(a n) -> a n", a=1).broadcast_to([P, D])))
    return loads


def attention(m, tag, dh, cross, g, b, wq, wk, wv, wo, bo, context, x_loads=()):
    nc = m.nc
    small = dh < 32
    NK = CTX_TOK if cross else TOK
    TILES = GROUPS if small else HEADS * dh // P
    inner = HEADS * dh
    scale = float(dh) ** -0.5
    VCH = inner if small else inner // GROUPS
    KD = CTX_D if cross else MAIN

    wo_tiles = m.wo[:, 0:TILES, :]
    loads = norm_loads(m, g, b, bo)
    fills = []
    if small:
        fills.append(wo_tiles)
        for j in range(GROUP):
            loads.append((m.wo[32 * j:32 * j + dh, 0:TILES, :], wo.rearrange("(g j d) n -> j d g n", g=GROUPS, j=GROUP)[j]))
    else:
        loads.append((wo_tiles, wo.rearrange("(t p) n -> p t n", p=P)))
    prepare_weights(m, tag + "w", [(wq, m.wparts[0], inner, scale, small), (wk, m.wparts[1], inner, 1.0, small),
                                   (wv, m.wparts[2], inner, 1.0, False)], loads, fills, x_loads)

    with ExitStack() as ctx:
        sb = lambda name, shape, dt=F32: ctx.enter_context(nc.sbuf_tensor(f"{tag}_{name}", shape, dt))
        sem = lambda name: m.semaphore(ctx, f"{tag}_{name}")
        bank = lambda name: ctx.enter_context(nc.psum_tensor(f"{tag}_{name}_bank", [P, 512], F32))
        packed = small or cross
        scores_banks = ctx.enter_context(nc.psum_tensor(f"{tag}_scores_banks", [P, 2, 512], F32))
        SCORES_LAG = 1 if packed else 0

        def head_scores(k, j):
            bank, col = (k % 2, j * NK) if packed else (j % 2, (j // 2) * NK)
            return scores_banks[:, bank, col:col + NK]

        pt_bank, out_bank, qk_bank, v_bank, y_bank, h_bank = (bank(x) for x in ("pt", "out", "qk", "v", "y", "h"))
        s_ctx_high = sem("ctx_high")
        s_ctx_split = sem("ctx_split")
        norm = Norm(m, ctx, tag, h_bank, (lambda n: (s_ctx_split, n)) if cross else (lambda n: (s_ctx_split, 0)))
        if small:
            qstack = [sb(f"qstack{i}", [P, TILES, PAIR * P], F32R) for i in range(2)]
            kstack = sb("kstack", [P, TILES, PAIR * NK], F32R)
            kblocks = [sb(f"kblocks{i}", [P, TILES, PAIR, GROUP * NK], F32R) for i in range(2)]
            qk_high = [sb(f"qk_high{i}", [P, 512], F32R) for i in range(2)]
        else:
            qk = [sb(f"qk{i}", [P, TILES, PAIR * P + PAIR * NK * (2 if cross else 1)]) for i in range(2)]
        VW = 32 if small else dh
        v = [sb(f"v{i}", [P, HEADS, VW]) for i in range(4)]
        probs = [sb(f"probs{i}", [P, GROUP, NK]) for i in range(4)]
        negmax = [sb(f"negmax{i}", [P, GROUP]) for i in range(4)]
        sums = [sb(f"sums{i}", [P, GROUP]) for i in range(4)]
        rsums = [sb(f"rsums{i}", [P, GROUP]) for i in range(4)]
        probsT = [sb(f"probsT{i}", [P, GROUP, P]) for i in range(2)]
        OT = 1 if small else 2
        outT = [sb(f"outT{i}", [P, OT * P]) for i in range(2)]
        if cross:
            ctx_in = [sb(f"ctx_in{i}", [P, PAIR, CTX_D]) for i in range(2)]
            ctx_high = [sb(f"ctx_high{i}", [P, PAIR * NK], F32R) for i in range(2)]
            ctx_low = [sb(f"ctx_low{i}", [P, PAIR * NK], F32R) for i in range(2)]

        s_ctx = [sem(f"ctx_in{i}") for i in range(2)]
        s_ctxT = sem("ctxT")
        s_scores = sem("scores")
        s_negmax = sem("negmax_ready")
        s_exp = sem("exp")
        s_rsums = sem("rsums_ready")
        s_probs = sem("probs_ready")
        s_pt = sem("pt")
        s_probsT = sem("probsT_ready")
        s_out = sem("heads_out")
        s_outT = sem("outT_ready")
        s_wo = sem("wo")
        s_resid = sem("resid")
        s_qkproj = sem("qkproj")
        s_qkhigh = sem("qkhigh")
        s_qk = sem("qk_ready")
        s_kblocks = [sem(f"kblocks{i}_ready") for i in range(2)]
        s_vproj = sem("vproj")
        s_v = sem("v_ready")
        s_zero = sem("zeroed")
        zeroed = [t[:] for t in kblocks + v] if small else [t[:, :, PAIR * P:] for t in qk] if cross else []
        VN = PAIR if small else PSTEPS
        ctx.callback(m.end_stage)
        block = ctx.enter_context(nc.Block())

        number = lambda q, k: q * QSTEPS + k
        pair_of = lambda q, k: q * 2 + k // PSTEPS
        seq_of = lambda q, k: q * 4 + k // GROUPS

        def tile_at(q, k):
            s = k % PSTEPS
            if not live(pair_of(q, k) + 1, PAIRS):
                return None
            return s, (k // PSTEPS + 1) % 2, (pair_of(q, k) + 1) * PSTEPS + s

        def chunk_at(q, k):
            s = k % PSTEPS
            if not live(pair_of(q, k) + 1, PAIRS):
                return None
            if small:
                if s not in (GROUPS, GROUPS + 1):
                    return None
                a, c = s - GROUPS, 0
            else:
                a, c = s // GROUPS, s % GROUPS
            return a, c, (2 * (k // PSTEPS + 1) + a) % 4, (pair_of(q, k) + 1) * VN + (a if small else s)

        def run(engine, step):
            for k in range(-2 * PSTEPS, QSTEPS):
                step(0, k)
            with engine.Fori(1, QUADS - 1) as q:
                for k in range(QSTEPS):
                    step(q, k)
            for k in range(QSTEPS + 6):
                step(QUADS - 1, k)

        @block.sync
        def _(sp):
            def step(q, k):
                n, ahead = number(q, k), pair_of(q, k) + 2
                if cross and k % PSTEPS == 0 and live(ahead, PAIRS):
                    par = (k // PSTEPS) % 2
                    source = context(address(sp, q * 4 + 2 * (k // PSTEPS) + 4))
                    if due(ahead - 1):
                        sp.wait_ge(s_ctxT, ahead - 1)
                    sp.dma_start(ctx_in[par][0:NK, :, :], source).then_inc(s_ctx[par], 16)
                if small and k % PSTEPS == GROUPS and live(ahead - 1, PAIRS):
                    par = (k // PSTEPS + 1) % 2
                    if isinstance(n, int) and n < 0:
                        sp.wait_ge(s_zero, len(zeroed))
                    if due((ahead - 1) * PSTEPS + GROUPS):
                        sp.wait_ge(s_qk, (ahead - 1) * PSTEPS + GROUPS)
                    for j in range(GROUP):
                        rows = slice(32 * j, 32 * j + 32)
                        sp.dma_start(kblocks[par][rows, :, :, j * NK:(j + 1) * NK].bitcast(F32),
                                     kstack[rows, :, :].bitcast(F32).rearrange("p t (a k) -> p t a k", a=PAIR)).then_inc(s_kblocks[par], 16)

            run(sp, step)

        @block.gpsimd
        def _(pool):
            for t in zeroed:
                nc.gpsimd.memset(t.bitcast(F32) if t.dtype == F32R else t, 0.0).then_inc(s_zero, 1)

            def step(q, k):
                n, s, ahead = number(q, k), k % PSTEPS, pair_of(q, k) + 2
                if s == 1 and live(ahead, PAIRS):
                    norm.gpsimd_rstd(pool, ahead)
                if s == 3 and live(ahead, PAIRS):
                    norm.gpsimd_bias(pool, ahead, q * 4 + 2 * (k // PSTEPS) + 4)
                if live(n - 1, STEPS):
                    i = (k - 1) % 4
                    if due(n):
                        pool.wait_ge(s_rsums, n)
                    nc.gpsimd.tensor_tensor(probs[i][:], probs[i][:], rsums[i][:].unsqueeze(2).broadcast_to([P, GROUP, NK]),
                                            ALU.mult).then_inc(s_probs, 1)

            run(pool, step)

        @block.scalar
        def _(act):
            def step(q, k):
                n, s, ahead = number(q, k), k % PSTEPS, pair_of(q, k) + 2
                tile = tile_at(q, k)
                if tile and small:
                    t, par, r = tile
                    width = PAIR * NK if t < GROUPS else PAIR * P
                    if due(r + 1):
                        act.wait_ge(s_qkproj, r + 1)
                    if due(r - 1):
                        act.wait_ge(s_qk, r - 1)
                    nc.scalar.copy(qk_high[t % 2][:, 0:width], qk_bank[:, 0:width]).then_inc(s_qkhigh, 1)
                if live(n, STEPS):
                    i = k % 4
                    if due(n + 1):
                        act.wait_ge(s_negmax, n + 1)
                    if due(n - 3):
                        act.wait_ge(s_pt, n - 3)
                    for j in range(GROUP):
                        last = nc.scalar.activation(probs[i][:, j, :], head_scores(k, j), ACT.Exp,
                                                    bias=negmax[i][:, j:j + 1], scale=1.0, accum_out=sums[i][:, j:j + 1])
                    last.then_inc(s_exp, 1)
                if tile and not small:
                    t, par, r = tile
                    if due(r + 1):
                        act.wait_ge(s_qkproj, r + 1)
                    if due(n):
                        act.wait_ge(s_scores, n)
                    if cross:
                        if isinstance(n, int) and n < 0:
                            act.wait_ge(s_zero, len(zeroed))
                        nc.scalar.copy(qk[par][:, t, 0:PAIR * P], qk_bank[:, 0:PAIR * P])
                        for half in range(2):
                            rows = slice(half * dh, (half + 1) * dh)
                            last = nc.scalar.copy(
                                qk[par][rows, t, PAIR * P:].rearrange("p (a b k) -> p a b k", a=PAIR, b=2)[:, :, half, :],
                                qk_bank[rows, PAIR * P:PAIR * P + PAIR * NK].rearrange("p (a k) -> p a k", a=PAIR))
                        last.then_inc(s_qk, 1)
                    else:
                        nc.scalar.copy(qk[par][:, t, :], qk_bank[:, :]).then_inc(s_qk, 1)
                if small and live(n - 4, STEPS):
                    i = (k - 4) % 2
                    if due(n - 3):
                        act.wait_ge(s_out, n - 3)
                    if due(n - 5):
                        act.wait_ge(s_wo, n - 5)
                    nc.scalar.copy(outT[i][:], out_bank[:, 0:OT * P]).then_inc(s_outT, 1)
                chunk = chunk_at(q, k)
                if chunk:
                    a, c, slot, r = chunk
                    if due(r + 1):
                        act.wait_ge(s_vproj, r + 1)
                    if due((pair_of(q, k) - 1) * PSTEPS + (a + 1) * GROUPS):
                        act.wait_ge(s_out, (pair_of(q, k) - 1) * PSTEPS + (a + 1) * GROUPS)
                    if small:
                        if isinstance(n, int) and n < 0:
                            act.wait_ge(s_zero, len(zeroed))
                        nc.scalar.copy(v[slot][0:NK, :, 0:dh], v_bank[0:NK, 0:inner].rearrange("p (h d) -> p h d", h=HEADS))\
                            .then_inc(s_v, 1)
                    else:
                        nc.scalar.copy(v[slot][0:NK, c * GROUP:(c + 1) * GROUP, :],
                                       v_bank[0:NK, 0:VCH].rearrange("p (h d) -> p h d", h=GROUP)).then_inc(s_v, 1)
                if s == 4 and live(ahead, PAIRS):
                    norm.scalar_affine(act, ahead, (k // PSTEPS) % 2, (s_vproj, (ahead - 1) * VN))
                if cross and s == 6 and live(ahead, PAIRS):
                    par = (k // PSTEPS) % 2
                    if due(ahead + 1):
                        act.wait_ge(s_ctxT, ahead + 1)
                    if due((ahead - 1) * VN):
                        act.wait_ge(s_vproj, (ahead - 1) * VN)
                    nc.scalar.copy(ctx_high[par][0:CTX_D, :], h_bank[0:CTX_D, 0:PAIR * NK]).then_inc(s_ctx_high, 1)

            run(act, step)

        @block.vector
        def _(dve):
            def step(q, k):
                n, s, ahead = number(q, k), k % PSTEPS, pair_of(q, k) + 2
                seq_ahead = q * 4 + 2 * (k // PSTEPS) + 4
                if s == 1 and live(ahead, PAIRS):
                    norm.wait_stats(dve, ahead)
                if live(n, STEPS):
                    if due(n + 1):
                        dve.wait_ge(s_scores, n + 1)
                    if due(n - 3):
                        dve.wait_ge(s_exp, n - 3)
                    if packed:
                        heads, best = scores_banks[:, k % 2, 0:GROUP * NK].rearrange("p (h k) -> p h k", h=GROUP), negmax[k % 4][:]
                    else:
                        heads = scores_banks[:, :, 0:2 * NK].rearrange("p b (c k) -> p b c k", c=2)
                        best = negmax[k % 4][:].rearrange("p (c b) -> p b c", b=2)
                    nc.vector.tensor_reduce(out=best, in_=heads, axis=AX.X, op=ALU.max, negate=True).then_inc(s_negmax, 1)
                if s == 1 and live(ahead, PAIRS):
                    norm.vector_moments(dve, ahead)
                if live(n - 1, STEPS):
                    i = (k - 1) % 4
                    if due(n):
                        dve.wait_ge(s_exp, n)
                    if due(n - 4):
                        dve.wait_ge(s_probs, n - 4)
                    nc.vector.reciprocal(rsums[i][:], sums[i][:]).then_inc(s_rsums, 1)
                tile = tile_at(q, k)
                if tile and small:
                    t, par, r = tile
                    if due(r + 1):
                        dve.wait_ge(s_qkhigh, r + 1)
                    if s == 0:
                        if due(16 * GROUP * half(q, k)):
                            dve.wait_ge(s_kblocks[(par + 1) % 2], 16 * GROUP * half(q, k))
                    width = PAIR * NK if t < GROUPS else PAIR * P
                    stack, minus = (kstack, m.minus_last8) if t < GROUPS else (qstack[par], m.minus_low8)
                    nc.vector.scalar_tensor_tensor(out=stack[:, t % GROUPS, :], in0=qk_high[t % 2][:, 0:width].bitcast(F32),
                                                   scalar=minus[:, 0:1], in1=qk_bank[:, 0:width], op0=ALU.mult,
                                                   op1=ALU.add).then_inc(s_qk, 1)
                if live(n - 3, STEPS):
                    i = (k - 3) % 2
                    if due(n - 2):
                        dve.wait_ge(s_pt, n - 2)
                    if due(n - 4):
                        dve.wait_ge(s_out, n - 4)
                    nc.vector.tensor_copy(probsT[i][0:NK, :, :], pt_bank[0:NK, :].rearrange("p (h k) -> p h k", h=GROUP))\
                        .then_inc(s_probsT, 1)
                if not small and live(n - 4, STEPS):
                    i = (k - 4) % 2
                    if due(n - 3):
                        dve.wait_ge(s_out, n - 3)
                    if due(n - 5):
                        dve.wait_ge(s_wo, n - 5)
                    nc.vector.tensor_copy(outT[i][:], out_bank[:, 0:OT * P]).then_inc(s_outT, 1)
                if live(n - 5, STEPS) and (k - 5) % GROUPS == GROUPS - 1:
                    seq = seq_of(q, k - 5)
                    if due(n - 4):
                        dve.wait_ge(s_wo, n - 4)
                    if due(pair_of(q, k - 5) + 1):
                        dve.wait_ge(norm.s_biased, pair_of(q, k - 5) + 1)
                    xt = m.x1(seq)
                    nc.vector.tensor_tensor(xt, y_bank[:, 0:D], xt, ALU.add).then_inc(s_resid, 1)
                if s == 0 and live(ahead, PAIRS):
                    norm.vector_stats(dve, ahead, seq_ahead)
                if s == 2 and live(ahead, PAIRS):
                    norm.vector_h(dve, ahead, seq_ahead)
                if s == 5 and live(ahead, PAIRS):
                    norm.vector_split(dve, ahead, (k // PSTEPS) % 2)
                if cross and s == 7 and live(ahead, PAIRS):
                    par = (k // PSTEPS) % 2
                    if due(ahead + 1):
                        dve.wait_ge(s_ctx_high, ahead + 1)
                    nc.vector.tensor_tensor(ctx_low[par][0:CTX_D, :], h_bank[0:CTX_D, 0:PAIR * NK],
                                            ctx_high[par][0:CTX_D, :].bitcast(F32), ALU.subtract).then_inc(s_ctx_split, 1)

            def half(q, k):
                return q + (k // PSTEPS + 1) // 2 if (k // PSTEPS + 1) % 2 == 0 else q + (k // PSTEPS + 1 + 1) // 2

            run(dve, step)

        @block.tensor
        def _(pe):
            def step(q, k):
                n, s, ahead = number(q, k), k % PSTEPS, pair_of(q, k) + 2
                a, grp = (k % PSTEPS) // GROUPS, k % GROUPS
                par = (k // PSTEPS) % 2
                if live(n, STEPS):
                    if due(n - SCORES_LAG):
                        pe.wait_ge(s_exp, n - SCORES_LAG)
                    if s == 0:
                        if small:
                            pe.wait_ge(s_kblocks[par], (q + 1) * (16 * GROUP))
                        pe.wait_ge(s_qk, (pair_of(q, k) + 1) * PSTEPS)
                    if small:
                        last = nc.tensor.matmul(scores_banks[:, k % 2, 0:GROUP * NK], qstack[par][:, grp, a * P:(a + 1) * P],
                                                kblocks[par][:, grp, a, :], start=True, stop=True)
                    elif cross:
                        for c in range(GROUP // 2):
                            t = 2 * grp + c
                            last = nc.tensor.matmul(scores_banks[:, k % 2, c * 2 * NK:(c + 1) * 2 * NK], qk[par][:, t, a * P:(a + 1) * P],
                                                    qk[par][:, t, PAIR * P + a * 2 * NK:PAIR * P + (a + 1) * 2 * NK],
                                                    start=True, stop=True)
                    else:
                        for j in range(GROUP):
                            rows, t = slice(dh * (j % 2), dh * (j % 2) + dh), 2 * grp + j // 2
                            last = nc.tensor.matmul(head_scores(k, j), qk[par][rows, t, a * P:(a + 1) * P],
                                                    qk[par][rows, t, PAIR * P + a * NK:PAIR * P + (a + 1) * NK], start=True, stop=True)
                    last.then_inc(s_scores, 1)
                tile = tile_at(q, k)
                if tile:
                    t, tpar, r = tile
                    if s == 0:
                        if due(ahead):
                            pe.wait_ge(norm.s_split, ahead)
                        if cross:
                            if due(ahead):
                                pe.wait_ge(s_ctx_split, ahead)
                    if due(r):
                        pe.wait_ge(s_qk, r)
                    cols = slice(t % TILES * P, (t % TILES + 1) * P)
                    (qh, ql, qs), (kh, kl, ks) = m.wparts[0], m.wparts[1]
                    hh, hl, hs = norm.high[tpar][:], norm.low[tpar][:], norm.stack[tpar][0:STACK, :]
                    if not small or t >= GROUPS:
                        last = products(nc, qk_bank[:, 0:PAIR * P],
                                        [(qh[:, cols], hh), (qh[:, cols], hl), (ql[:, cols], hh), (qs[0:STACK, cols], hs)])
                    kcol = 0 if small else PAIR * P
                    kout = qk_bank[:, kcol:kcol + PAIR * NK]
                    if small and t >= GROUPS:
                        pass
                    elif cross:
                        ch, cl = ctx_high[tpar][0:CTX_D, :], ctx_low[tpar][0:CTX_D, :]
                        last = products(nc, kout, [(kh[0:CTX_D, cols], ch), (kh[0:CTX_D, cols], cl), (kl[0:CTX_D, cols], ch)])
                    else:
                        last = products(nc, kout, [(kh[:, cols], hh), (kh[:, cols], hl), (kl[:, cols], hh), (ks[0:STACK, cols], hs)])
                    last.then_inc(s_qkproj, 1)
                if live(n - 3, STEPS):
                    if due(n - 2):
                        pe.wait_ge(s_probs, n - 2)
                    if due(n - 3):
                        pe.wait_ge(s_probsT, n - 3)
                    for j in range(GROUP):
                        last = nc.tensor.transpose(pt_bank[0:NK, j * P:(j + 1) * P], probs[(k - 3) % 4][:, j, :], m.ident[:])
                    last.then_inc(s_pt, 1)
                chunk = chunk_at(q, k)
                if chunk:
                    ca, c, slot, r = chunk
                    tpar = (k // PSTEPS + 1) % 2
                    if due(r):
                        pe.wait_ge(s_v, r)
                    cols = slice(c * VCH, (c + 1) * VCH)
                    vh, vl, vs = m.wparts[2]
                    if cross:
                        tok = slice(ca * NK, (ca + 1) * NK)
                        ch, cl = ctx_high[tpar][0:CTX_D, tok], ctx_low[tpar][0:CTX_D, tok]
                        last = products(nc, v_bank[0:NK, 0:VCH],
                                        [(ch, vh[0:CTX_D, cols]), (ch, vl[0:CTX_D, cols]), (cl, vh[0:CTX_D, cols])])
                    else:
                        tok = slice(ca * P, (ca + 1) * P)
                        hh, hl, hs = norm.high[tpar][:, tok], norm.low[tpar][:, tok], norm.stack[tpar][0:STACK, tok]
                        last = products(nc, v_bank[:, 0:VCH],
                                        [(hh, vh[:, cols]), (hh, vl[:, cols]), (hl, vh[:, cols]), (hs, vs[0:STACK, cols])])
                    last.then_inc(s_vproj, 1)
                if live(n - 4, STEPS):
                    if due(n - 3):
                        pe.wait_ge(s_probsT, n - 3)
                    if due(n - 4):
                        pe.wait_ge(s_outT, n - 4)
                    g3, slot = (k - 4) % GROUPS, ((k - 4) // GROUPS) % 4
                    if g3 == 0:
                        if small:
                            pe.wait_ge(s_v, seq_of(q, k - 4) + 1)
                        else:
                            pe.wait_ge(s_v, (seq_of(q, k - 4) + 1) * GROUPS)
                    for j in range(GROUP):
                        rows, col = (32 * j, 0) if small else (dh * (j % 2), j // 2)
                        last = nc.tensor.matmul(out_bank[rows:rows + VW, col * P:(col + 1) * P], v[slot][0:NK, g3 * GROUP + j, :],
                                                probsT[(k - 4) % 2][0:NK, j, :], start=True, stop=True)
                    last.then_inc(s_out, 1)
                if live(n - 5, STEPS):
                    g4 = (k - 5) % GROUPS
                    if due(n - 4):
                        pe.wait_ge(s_outT, n - 4)
                    if g4 == 0:
                        if due(seq_of(q, k - 5)):
                            pe.wait_ge(s_resid, seq_of(q, k - 5))
                    for t in range(OT):
                        last = nc.tensor.matmul(y_bank[:, 0:D], outT[(k - 5) % 2][:, t * P:(t + 1) * P], m.wo[:, g4 * OT + t, :],
                                                start=(g4 == 0 and t == 0), stop=(g4 == GROUPS - 1 and t == OT - 1))
                    last.then_inc(s_wo, 1)
                if s == 4 and live(ahead, PAIRS):
                    norm.tensor_transpose(pe, ahead)
                if cross and s == 6 and live(ahead, PAIRS):
                    cpar = (k // PSTEPS) % 2
                    if due(ahead * 2 + 2):
                        pe.wait_ge(norm.s_y, ahead * 2 + 2)
                    pe.wait_ge(s_ctx[cpar], (q + (k // PSTEPS + 2) // 2 + 1) * 16 if cpar == 0 else (q + (k // PSTEPS + 1) // 2 + 1) * 16)
                    for b2 in range(PAIR):
                        last = nc.tensor.transpose(h_bank[0:CTX_D, b2 * NK:(b2 + 1) * NK], ctx_in[cpar][0:NK, b2, :], m.ident[0:NK, 0:NK])
                    last.then_inc(s_ctxT, 1)

            run(pe, step)


def feed_forward(m, tag, gelu, g, b, w1, b1, w2, b2, out=None):
    nc = m.nc
    TILES = FF // P
    bias1 = m.bias1
    loads = norm_loads(m, g, b, b2)
    loads.append((bias1[:], b1.rearrange("(t p) -> p t", p=P)))
    loads.append((m.wo[:, 0:TILES, :], w2.rearrange("(t p) n -> p t n", p=P)))
    prepare_weights(m, tag + "w", [(w1, m.wparts[0], 2 * FF, 1.0, False)], loads)
    with ExitStack() as ctx:
        sb = lambda name, shape, dt=F32: ctx.enter_context(nc.sbuf_tensor(f"{tag}_{name}", shape, dt))
        sem = lambda name: m.semaphore(ctx, f"{tag}_{name}")
        bank = lambda name: ctx.enter_context(nc.psum_tensor(f"{tag}_{name}_bank", [P, 512], F32))
        up_bank = [bank(f"up{i}") for i in range(2)]
        y_bank = [[bank(f"y{i}{a}") for a in range(PAIR)] for i in range(2)]
        h_bank = bank("h")
        s_never = sem("unused")
        norm = Norm(m, ctx, tag, h_bank, lambda n: (s_never, 0))
        gate = [sb(f"gate{i}", [P, PAIR * P]) for i in range(2)]
        act_t = [sb(f"hidden{i}", [P, PAIR * P]) for i in range(2)]
        s_up = sem("up")
        s_gate = sem("gate_ready")
        s_hidden = sem("hidden_ready")
        s_down = sem("down")
        s_resid = sem("resid")
        s_store = sem("store")
        ctx.callback(m.end_stage)
        block = ctx.enter_context(nc.Block())
        BODY = 2 * TILES
        number = lambda q, k: q * BODY + k
        pair_of = lambda q, k: q * 2 + k // TILES
        TOTAL = PAIRS * TILES

        def run(engine, step):
            for k in range(-2 * TILES, BODY):
                step(0, k)
            with engine.Fori(1, QUADS - 1) as q:
                for k in range(BODY):
                    step(q, k)
            for k in range(BODY + 4):
                step(QUADS - 1, k)

        @block.sync
        def _(sp):
            if out is None:
                return

            def step(q, k):
                n = number(q, k)
                if (k - 3) % TILES == TILES - 1 and live(n - 3, TOTAL):
                    seq = address(sp, q * 4 + 2 * ((k - 3) // TILES))
                    if due(pair_of(q, k - 3) + 1):
                        sp.wait_ge(s_resid, pair_of(q, k - 3) + 1)
                    sp.dma_start(out[bass.ds(seq, PAIR), :, :].rearrange("s p d -> p s d"), m.xpair(seq)).then_inc(s_store, 16)

            run(sp, step)
            sp.wait_ge(s_store, 16 * PAIRS)

        @block.gpsimd
        def _(pool):
            def step(q, k):
                s, ahead = k % TILES, pair_of(q, k) + 2
                if live(ahead, PAIRS):
                    if s == 1:
                        norm.gpsimd_rstd(pool, ahead)
                    if s == 4:
                        norm.gpsimd_bias(pool, ahead, q * 4 + 2 * (k // TILES) + 4)

            run(pool, step)

        @block.scalar
        def _(act):
            def step(q, k):
                n, s, ahead = number(q, k), k % TILES, pair_of(q, k) + 1
                if live(n, TOTAL):
                    if due(n + 1):
                        act.wait_ge(s_up, n + 1)
                    if due(n - 1):
                        act.wait_ge(s_hidden, n - 1)
                    nc.scalar.activation(gate[k % 2][:], up_bank[k % 2][:, PAIR * P:], gelu,
                                         bias=bias1[:, TILES + s:TILES + s + 1], scale=1.0).then_inc(s_gate, 1)
                if s == 1 and live(ahead, PAIRS):
                    norm.scalar_affine(act, ahead, (k // TILES + 1) % 2, (s_up, (ahead - 1) * TILES))

            run(act, step)

        @block.vector
        def _(dve):
            def step(q, k):
                n, s, ahead = number(q, k), k % TILES, pair_of(q, k) + 2
                seq_ahead = q * 4 + 2 * (k // TILES) + 4
                if s == 1 and live(ahead, PAIRS):
                    norm.wait_stats(dve, ahead)
                if live(n, TOTAL):
                    if due(n + 1):
                        dve.wait_ge(s_gate, n + 1)
                    if due(n - 1):
                        dve.wait_ge(s_down, n - 1)
                    nc.vector.scalar_tensor_tensor(out=act_t[k % 2][:], in0=up_bank[k % 2][:, 0:PAIR * P],
                                                   scalar=bias1[:, s:s + 1], in1=gate[k % 2][:], op0=ALU.add,
                                                   op1=ALU.mult).then_inc(s_hidden, 1)
                if (k - 3) % TILES == TILES - 1 and live(n - 3, TOTAL):
                    seq, ypar = q * 4 + 2 * ((k - 3) // TILES), ((k - 3) // TILES) % 2
                    if due(n - 2):
                        dve.wait_ge(s_down, n - 2)
                    if due(pair_of(q, k - 3) + 1):
                        dve.wait_ge(norm.s_biased, pair_of(q, k - 3) + 1)
                    for a in range(PAIR):
                        xt = m.xs(seq, a)
                        last = nc.vector.tensor_tensor(xt, y_bank[ypar][a][:, 0:D], xt, ALU.add)
                    last.then_inc(s_resid, 1)
                if live(ahead, PAIRS):
                    if s == 0:
                        norm.vector_stats(dve, ahead, seq_ahead)
                    if s == 1:
                        norm.vector_moments(dve, ahead)
                    if s == 3:
                        norm.vector_h(dve, ahead, seq_ahead)
                if s == 2 and live(ahead - 1, PAIRS):
                    norm.vector_split(dve, ahead - 1, (k // TILES + 1) % 2)

            run(dve, step)

        @block.tensor
        def _(pe):
            def step(q, k):
                n, s, ahead = number(q, k), k % TILES, pair_of(q, k) + 1
                par = (k // TILES) % 2
                if live(n, TOTAL):
                    if s == 0:
                        pe.wait_ge(norm.s_split, pair_of(q, k) + 1)
                    if due(n - 1):
                        pe.wait_ge(s_hidden, n - 1)
                    wh, wl, ws = m.wparts[0]
                    hh, hl, hs = norm.high[par][:], norm.low[par][:], norm.stack[par][0:STACK, :]
                    for half in range(2):
                        cols = slice(half * FF + s * P, half * FF + (s + 1) * P)
                        last = products(nc, up_bank[k % 2][:, half * PAIR * P:(half + 1) * PAIR * P],
                                        [(wh[:, cols], hh), (wh[:, cols], hl), (wl[:, cols], hh), (ws[0:STACK, cols], hs)])
                    last.then_inc(s_up, 1)
                if live(n - 2, TOTAL):
                    t, ypar = (k - 2) % TILES, ((k - 2) // TILES) % 2
                    if due(n - 1):
                        pe.wait_ge(s_hidden, n - 1)
                    if t == 0:
                        if due(pair_of(q, k - 2) - 1):
                            pe.wait_ge(s_resid, pair_of(q, k - 2) - 1)
                    for a in range(PAIR):
                        last = nc.tensor.matmul(y_bank[ypar][a][:, 0:D], act_t[k % 2][:, a * P:(a + 1) * P], m.wo[:, t, :],
                                                start=(t == 0), stop=(t == TILES - 1))
                    last.then_inc(s_down, 1)
                if s == 0 and live(ahead, PAIRS):
                    norm.tensor_transpose(pe, ahead)

            run(pe, step)


def build(nc, A, out):
    m = Machine(nc)
    with ExitStack() as ctx:
        sb = lambda name, shape, dt=F32: ctx.enter_context(nc.sbuf_tensor(name, shape, dt))
        m.x = sb("x_tokens", [P, SEQS * D])
        m.wparts = [[sb(f"w{i}_{part}", [P, 1280], F32R) for part in ("high", "low", "stack")] for i in range(3)]
        m.wo = sb("w_out", [P, 10, D])
        m.norm_cols = sb("norm_cols", [P, 4])
        m.out_bias = sb("out_bias", [P, D])
        m.bias1 = sb("bias1", [P, 2 * FF // P])
        m.ident = sb("ident", [P, P])
        m.eps = sb("eps", [P, PAIR])
        m.minus_half = sb("minus_half", [P, PAIR])
        m.minus_low_row = sb("minus_low_row", [P, 1])
        m.minus_last_row = sb("minus_last_row", [P, 1])
        m.minus_low8 = sb("minus_low8", [P, 1])
        m.minus_last8 = sb("minus_last8", [P, 1])
        m.scrap = sb("scrap", [P, 4])
        band = sb("band", [P, 2, GROUP])
        m.x1 = lambda seq: m.x[:, bass.ds(seq * D, D)]
        m.xs = lambda seq, a: m.x[:, bass.ds(seq * D + a * D, D)]
        m.xpair = lambda seq: m.x[:, bass.ds(seq * D, PAIR * D)].rearrange("p (a d) -> p a d", a=PAIR)

        with ExitStack() as c0:
            s_pool = m.semaphore(c0, "const_pool")
            c0.callback(m.end_stage)
            block = c0.enter_context(nc.Block())

            @block.gpsimd
            def _(pool):
                made = [0]

                def link(instruction):
                    made[0] += 1
                    instruction.then_inc(s_pool, 1)
                    pool.wait_ge(s_pool, made[0])

                link(nc.gpsimd.memset(m.ident[:], 0.0))
                link(nc.gpsimd.affine_select(out=m.ident[:], in_=m.ident[:], compare_op=ALU.not_equal, fill=1.0, base=0,
                                             pattern=[[-1, P]], channel_multiplier=1))
                link(nc.gpsimd.memset(m.minus_half[:], -0.5))
                link(nc.gpsimd.memset(m.eps[:], EPS))
                for tile, row in ((m.minus_low_row, 1), (m.minus_last_row, 2)):
                    link(nc.gpsimd.memset(tile[:], 0.0))
                    link(nc.gpsimd.memset(tile[row * REM:(row + 1) * REM, :], -1.0))
                link(nc.gpsimd.memset(band[:], -1.0))
                for i in range(2):
                    lo = 8 * (i + 1)
                    link(nc.gpsimd.affine_select(out=band[:, i, :], in_=band[:, i, :], compare_op=ALU.is_ge, fill=0.0, base=-lo,
                                                 pattern=[[-32, GROUP]], channel_multiplier=1))
                    link(nc.gpsimd.affine_select(out=band[:, i, :], in_=band[:, i, :], compare_op=ALU.is_ge, fill=0.0,
                                                 base=lo + 7, pattern=[[32, GROUP]], channel_multiplier=-1))

            @block.vector
            def _(dve):
                dve.wait_ge(s_pool, 13)
                for i, tile in enumerate((m.minus_low8, m.minus_last8)):
                    nc.vector.tensor_reduce(out=tile[:], in_=band[:, i, :], axis=AX.X, op=ALU.add)

        x_in, c_in = A["x"], A["ctx_768"]
        context = lambda seq: c_in[bass.ds(seq, PAIR), :, :].rearrange("s p d -> p s d")
        CH = 4
        x_loads = [(m.x[:, i * CH * D:(i + 1) * CH * D].rearrange("p (s d) -> p s d", d=D),
                    x_in[i * CH:(i + 1) * CH, :, :].rearrange("s p d -> p s d")) for i in range(SEQS // CH)]
        L = lambda name: A["L0_xattn_" + name]
        attention(m, "a0", 8, False, L("n1_g"), L("n1_b"), L("q1"), L("k1"), L("v1"), L("o1_w"), L("o1_b"), context, x_loads)
        attention(m, "c0", 8, True, L("n2_g"), L("n2_b"), L("q2"), L("k2"), L("v2"), L("o2_w"), L("o2_b"), context)
        feed_forward(m, "f0", ACT.Gelu, L("n3_g"), L("n3_b"), L("ff_w1"), L("ff_b1"), L("ff_w2"), L("ff_b2"))
        L = lambda name: A["L1_xattn_" + name]
        attention(m, "a1", 64, False, L("g1"), L("be1"), L("wq1"), L("wk1"), L("wv1"), L("wo1"), L("bo1"), context)
        attention(m, "c1", 64, True, L("g2"), L("be2"), L("wq2"), L("wk2"), L("wv2"), L("wo2"), L("bo2"), context)
        feed_forward(m, "f1", ACT.Gelu_apprx_tanh, L("g3"), L("be3"), L("w_ff1"), L("b_ff1"), L("w_ff2"), L("b_ff2"), out)


def kernel(**inputs):
    import concourse.bacc as bacc
    from concourse.bass_utils import run_bass_kernel_spmd

    nc = bacc.Bacc("TRN2", target_bir_lowering=False, num_devices=1)
    arrays, A = {}, {}
    for name, value in inputs.items():
        a = np.ascontiguousarray(value)
        arrays[f"in_{name}"] = a
        A[name] = nc.dram_tensor(f"in_{name}", a.shape, mybir.dt.from_np(a.dtype), kind="ExternalInput").ap()
    out = nc.dram_tensor("out_x", (SEQS, TOK, D), F32, kind="ExternalOutput").ap()
    build(nc, A, out)
    result = run_bass_kernel_spmd(nc, [arrays], core_ids=[0])
    return result.results[0]["out_x"]
```

```python
import numpy as np
import concourse.bass as bass
from concourse import mybir
from contextlib import ExitStack

F32 = mybir.dt.float32
F32R = mybir.dt.float32r
ALU = mybir.AluOpType
ACT = mybir.ActivationFunctionType
AX = mybir.AxisListType

P = 128
SEQS, TOK, D = 64, 128, 160
CTX_TOK, CTX_D = 77, 96
HEADS = 20
FF = 640
MAIN = 128
REM = D - MAIN
STACK = 3 * REM
GROUP = 4
GROUPS = HEADS // GROUP
PAIR = 2
PSTEPS = PAIR * GROUPS
QSTEPS = 2 * PSTEPS
PAIRS = SEQS // PAIR
QUADS = SEQS // (2 * PAIR)
STEPS = SEQS * GROUPS
EPS = 1e-5


def live(value, total):
    return not isinstance(value, int) or 0 <= value < total


def due(count):
    return not isinstance(count, int) or count > 0


def address(engine, value):
    return value if isinstance(value, int) else engine.snap(value)


def clear(nc, semaphores):
    with nc.Block() as block:
        @block.sync
        def _(sp):
            for semaphore in semaphores:
                sp.sem_clear(semaphore)


class Machine:

    def __init__(self, nc):
        self.nc, self.stage_semaphores = nc, []
        self.tokens_wanted = None

    def semaphore(self, ctx, name):
        self.stage_semaphores.append(ctx.enter_context(self.nc.semaphore(name)))
        return self.stage_semaphores[-1]

    def end_stage(self):
        clear(self.nc, self.stage_semaphores)
        self.stage_semaphores = []


class Norm:

    def __init__(self, m, ctx, tag, bank, done_reading, params, weights):
        nc = m.nc
        self.params, self.weights = params, weights
        sb = lambda name, shape, dt=F32: ctx.enter_context(nc.sbuf_tensor(f"{tag}_{name}", shape, dt))
        sem = lambda name: m.semaphore(ctx, f"{tag}_{name}")
        self.m, self.bank, self.done_reading = m, bank, done_reading
        self.stats = sb("stats", [P, PAIR, 6])
        self.moments = sb("moments", [P, PAIR, 2])
        self.var_eps = sb("var_eps", [P, PAIR])
        self.rstd = sb("rstd", [P, PAIR])
        self.centred = sb("centred", [P, PAIR, D])
        self.h = sb("h", [P, PAIR, 2 * P])
        self.y = sb("y", [P, 2, PAIR * P])
        self.yhigh = sb("yhigh", [P, PAIR * P], F32R)
        self.high = [sb(f"high{i}", [P, PAIR * P], F32R) for i in range(2)]
        self.low = [sb(f"low{i}", [P, PAIR * P], F32R) for i in range(2)]
        self.stack = [sb(f"stack{i}", [P, PAIR * P], F32R) for i in range(2)]
        self.s_stats6 = sem("stats6")
        self.s_moments = sem("moments_ready")
        self.s_vareps = sem("var_eps_ready")
        self.s_rstd = sem("rstd_ready")
        self.s_centred = sem("centred")
        self.s_h = sem("h_ready")
        self.s_biased = sem("x_biased")
        self.s_hT = sem("hT_ready")
        self.s_y = sem("y_ready")
        self.s_high = sem("high_ready")
        self.s_split = sem("split_ready")

    def vector_stats(self, e, n, seq):
        nc, m = self.m.nc, self.m
        if m.tokens_wanted and isinstance(n, int) and n in (0, 2):
            semaphore, count = m.tokens_wanted[n // 2]
            e.wait_ge(semaphore, count)
        if due(n):
            e.wait_ge(self.s_h, n)
        for a in range(PAIR):
            nc.vector.bn_stats(self.stats[:, a, :], m.xs(seq, a)).then_inc(self.s_stats6, 1)

    def wait_stats(self, e, n):
        if due(n * PAIR + PAIR):
            e.wait_ge(self.s_stats6, n * PAIR + PAIR)

    def vector_moments(self, e, n):
        for a in range(PAIR):
            self.m.nc.vector.bn_aggr(self.moments[:, a, :], self.stats[:, a, :]).then_inc(self.s_moments, 1)

    def gpsimd_rstd(self, e, n):
        nc = self.m.nc
        if due(n * PAIR + PAIR):
            e.wait_ge(self.s_moments, n * PAIR + PAIR)
        nc.gpsimd.tensor_tensor(self.var_eps[:], self.moments[:, :, 1], self.m.eps[:], ALU.add).then_inc(self.s_vareps, 1)
        if due(n + 1):
            e.wait_ge(self.s_vareps, n + 1)
        nc.gpsimd.tensor_tensor(self.rstd[:], self.var_eps[:], self.m.minus_half[:], ALU.pow).then_inc(self.s_rstd, 1)

    def gpsimd_centre(self, e, n, seq):
        nc, m = self.m.nc, self.m
        nc.gpsimd.tensor_tensor(self.centred[:], m.xpair(seq), self.moments[:, :, 0:1].broadcast_to([P, PAIR, D]),
                                ALU.subtract).then_inc(self.s_centred, 1)

    def gpsimd_h(self, e, n):
        nc = self.m.nc
        if due(n + 1):
            e.wait_ge(self.s_rstd, n + 1)
        if due(n + 1):
            e.wait_ge(self.s_centred, n + 1)
        if due(n):
            e.wait_ge(self.s_hT, n)
        nc.gpsimd.tensor_tensor(self.h[:, :, 0:MAIN], self.centred[:, :, 0:MAIN],
                                self.rstd[:].unsqueeze(2).broadcast_to([P, PAIR, MAIN]), ALU.mult)
        nc.gpsimd.tensor_tensor(self.h[:, :, MAIN:].rearrange("p a (c d) -> p a c d", d=REM),
                                self.centred[:, :, MAIN:D].unsqueeze(2).broadcast_to([P, PAIR, 4, REM]),
                                self.rstd[:].unsqueeze(2).unsqueeze(3).broadcast_to([P, PAIR, 4, REM]),
                                ALU.mult).then_inc(self.s_h, 1)

    def gpsimd_bias(self, e, n, seq):
        nc, m = self.m.nc, self.m
        if isinstance(n, int) and n == 0:
            self.weights.wait_params(e)
        nc.gpsimd.tensor_tensor(m.xpair(seq), m.xpair(seq), self.params.out_bias[:].unsqueeze(1).broadcast_to([P, PAIR, D]),
                                ALU.add).then_inc(self.s_biased, 1)

    def tensor_transpose(self, e, n):
        nc = self.m.nc
        if due(n + 1):
            e.wait_ge(self.s_h, n + 1)
        if due(n * 2):
            e.wait_ge(self.s_y, n * 2)
        used, count = self.done_reading(n)
        if due(count):
            e.wait_ge(used, count)
        for part in range(2):
            for a in range(PAIR):
                last = nc.tensor.transpose(self.bank[:, part * PAIR * P + a * P: part * PAIR * P + (a + 1) * P],
                                           self.h[:, a, part * P:(part + 1) * P], self.m.ident[:])
        last.then_inc(self.s_hT, 1)

    def scalar_affine(self, e, n, par, parts_used):
        nc, m = self.m.nc, self.m
        if isinstance(n, int) and n == 0:
            self.weights.wait_params(e)
        if due(n + 1):
            e.wait_ge(self.s_hT, n + 1)
        if due(n):
            e.wait_ge(self.s_split, n)
        for part in range(2):
            nc.scalar.activation(self.y[:, part, :], self.bank[:, part * PAIR * P:(part + 1) * PAIR * P], ACT.Identity,
                                 bias=self.params.norm_cols[:, 2 * part + 1:2 * part + 2],
                                 scale=self.params.norm_cols[:, 2 * part:2 * part + 1]).then_inc(self.s_y, 1)
        if due(n * 2 + 2):
            e.wait_ge(self.s_y, n * 2 + 2)
        used, count = parts_used
        if due(count):
            e.wait_ge(used, count)
        nc.scalar.copy(self.high[par][:], self.y[:, 0, :]).then_inc(self.s_high, 1)
        nc.scalar.copy(self.yhigh[:], self.y[:, 1, :]).then_inc(self.s_high, 1)

    def vector_split(self, e, n, par):
        nc, m = self.m.nc, self.m
        if due(n * 2 + 2):
            e.wait_ge(self.s_high, n * 2 + 2)
        nc.vector.tensor_tensor(self.low[par][:], self.y[:, 0, :], self.high[par][:].bitcast(F32), ALU.subtract)
        nc.vector.scalar_tensor_tensor(out=self.stack[par][:], in0=self.yhigh[:].bitcast(F32), scalar=m.minus_low_row[:, 0:1],
                                       in1=self.y[:, 1, :], op0=ALU.mult, op1=ALU.add).then_inc(self.s_split, 1)


STAGE_WIDE = 1280


class Weights:

    def __init__(self, m, number, jobs, param_loads):
        self.m, self.jobs, self.param_loads = m, jobs, param_loads
        self.s_load = [m.ctx.enter_context(m.nc.semaphore(f"stage{number}_matrix{i}")) for i in range(len(jobs))]
        self.s_params = m.ctx.enter_context(m.nc.semaphore(f"stage{number}_params"))
        self.units = []
        for i, (src, parts, cols, scale, thrice) in enumerate(jobs):
            for part in range(2 if src.shape[0] == D else 1):
                self.units.append((i, part, STACK if part else min(MAIN, src.shape[0])))
        cols = jobs[0][2]
        self.narrow = cols < STAGE_WIDE // 2
        places = [m.staging[0][:, u * cols:(u + 1) * cols] for u in range(6)] if self.narrow else [t[:] for t in m.staging]
        self.plain = places[:len(self.units)]
        self.early = len(self.plain)

    def begin(self, ctx, tag, spare):
        m = self.m
        self.plain += spare[:len(self.units) - self.early]
        if self.narrow:
            self.spread, self.rem_high = m.staging[1:3], m.staging[3][:].bitcast(F32R)
        else:
            self.spread, self.rem_high = None, spare[-1].bitcast(F32R)
        self.s_scaled = m.semaphore(ctx, f"{tag}_scaled")
        self.s_high = m.semaphore(ctx, f"{tag}_high")
        self.s_rest = m.semaphore(ctx, f"{tag}_rest")
        self.s_zero = m.semaphore(ctx, f"{tag}_zero")

    def width(self, job):
        return GROUPS * P if job[4] else job[2]

    def changed(self, job):
        return job[4] or job[3] != 1.0

    def sync_loads(self, sp, first, last):
        for i, part, rows in self.units[first:last]:
            src, parts, cols, scale, thrice = self.jobs[i]
            place = self.plain[self.units.index((i, part, rows))]
            if part:
                for c in range(3):
                    sp.dma_start(place[c * REM:(c + 1) * REM, 0:cols], src[MAIN:D, :]).then_inc(self.s_load[i], 16)
            else:
                sp.dma_start(place[0:rows, 0:cols], src[0:rows, :]).then_inc(self.s_load[i], 16)

    def sync_params(self, sp):
        with self.m.nc.allow_non_contiguous_dma(reason="small parameters, one value per partition"):
            for dst, src in self.param_loads:
                sp.dma_start(dst, src).then_inc(self.s_params, 16)

    def wait_params(self, e):
        e.wait_ge(self.s_params, 16 * len(self.param_loads))

    def wait_split(self, e):
        e.wait_ge(self.s_rest, len(self.units))

    def scalar_high(self, act, u):
        i, part, rows = self.units[u]
        src, (high, low, stack), cols, scale, thrice = self.jobs[i]
        wide = self.width(self.jobs[i])
        if self.changed(self.jobs[i]):
            act.wait_ge(self.s_scaled, sum(self.changed(self.jobs[i2]) for i2, part2, rows2 in self.units[:u + 1]))
        else:
            act.wait_ge(self.s_load[i], 16 * (4 if src.shape[0] == D else 1))
        if part and u >= 2:
            act.wait_ge(self.s_rest, u - 1)
        w = self.spread[part] if thrice else self.plain[u]
        self.m.nc.scalar.copy((self.rem_high if part else high)[0:rows, 0:wide], w[0:rows, 0:wide]).then_inc(self.s_high, 1)

    def vector_rest(self, dve, u):
        nc = self.m.nc
        i, part, rows = self.units[u]
        src, (high, low, stack), cols, scale, thrice = self.jobs[i]
        wide = self.width(self.jobs[i])
        w = self.plain[u][0:rows, 0:cols]
        dve.wait_ge(self.s_load[i], 16 * (4 if src.shape[0] == D else 1))
        if thrice:
            t, dh = self.spread[part][0:rows, 0:wide], cols // HEADS
            if u >= 2:
                dve.wait_ge(self.s_rest, u - 1)
            nc.vector.memset(t, 0.0).then_inc(self.s_zero, 1)
            dve.wait_ge(self.s_zero, u + 1)
            nc.vector.tensor_scalar(
                t.rearrange("p (h c) -> p h c", h=HEADS)[:, :, 0:3 * dh].rearrange("p h (c d) -> p h c d", c=3),
                w.rearrange("p (h d) -> p h d", h=HEADS).unsqueeze(2).broadcast_to([rows, HEADS, 3, dh]),
                scale, None, ALU.mult).then_inc(self.s_scaled, 1)
            w = t
        elif scale != 1.0:
            nc.vector.tensor_scalar(w, w, scale, None, ALU.mult).then_inc(self.s_scaled, 1)
        dve.wait_ge(self.s_high, u + 1)
        if part:
            nc.vector.scalar_tensor_tensor(
                out=stack[0:rows, 0:wide], in0=self.rem_high[0:rows, 0:wide].bitcast(F32),
                scalar=self.m.minus_last_row[0:rows, 0:1], in1=w, op0=ALU.mult, op1=ALU.add).then_inc(self.s_rest, 1)
        else:
            nc.vector.tensor_tensor(low[0:rows, 0:wide], w, high[0:rows, 0:wide].bitcast(F32),
                                    ALU.subtract).then_inc(self.s_rest, 1)


def products(nc, out, pairs):
    for i, (stationary, moving) in enumerate(pairs):
        last = nc.tensor.matmul(out, stationary, moving, start=(i == 0), stop=(i == len(pairs) - 1))
    return last


class Params:

    def __init__(self, sb, i):
        self.norm_cols = sb(f"norm_cols{i}", [P, 4])
        self.out_bias = sb(f"out_bias{i}", [P, D])
        self.bias1 = sb(f"bias1_{i}", [P, 2 * FF // P])

    def loads(self, g, b, out_bias, b1=None):
        loads = []
        for c, v in ((0, g), (1, b)):
            col = v.rearrange("(n a) -> n a", a=1)
            loads.append((self.norm_cols[:, c:c + 1], col[0:MAIN, :]))
            loads += [(self.norm_cols[r * REM:(r + 1) * REM, c + 2:c + 3], col[MAIN:D, :]) for r in range(4)]
        loads.append((self.out_bias[:], out_bias.rearrange("(a n) -> a n", a=1).broadcast_to([P, D])))
        if b1 is not None:
            loads.append((self.bias1[:], b1.rearrange("(t p) -> p t", p=P)))
        return loads


def attention_weights(m, number, dh, params, g, b, wq, wk, wv, bo):
    inner, small = HEADS * dh, dh < 32
    return Weights(m, number, [(wq, m.wparts[0], inner, float(dh) ** -0.5, small), (wk, m.wparts[1], inner, 1.0, small),
                               (wv, m.wparts[2], inner, 1.0, False)], params.loads(g, b, bo))


def attention(m, tag, dh, cross, wo, context, params, weights, following):
    nc = m.nc
    small = dh < 32
    NK = CTX_TOK if cross else TOK
    TILES = GROUPS if small else HEADS * dh // P
    inner = HEADS * dh
    VCH = inner if small else inner // GROUPS
    wo_tiles = m.wo[:, 0:TILES, :]
    if small:
        wo_loads = [(m.wo[32 * j:32 * j + dh, 0:TILES, :], wo.rearrange("(g j d) n -> j d g n", g=GROUPS, j=GROUP)[j])
                    for j in range(GROUP)]
    else:
        wo_loads = [(wo_tiles, wo.rearrange("(t p) n -> p t n", p=P))]

    with ExitStack() as ctx:
        sb = lambda name, shape, dt=F32: ctx.enter_context(nc.sbuf_tensor(f"{tag}_{name}", shape, dt))
        sem = lambda name: m.semaphore(ctx, f"{tag}_{name}")
        bank = lambda name: ctx.enter_context(nc.psum_tensor(f"{tag}_{name}_bank", [P, 512], F32))
        packed = small or cross
        scores_banks = ctx.enter_context(nc.psum_tensor(f"{tag}_scores_banks", [P, 2, 512], F32))
        SCORES_LAG = 1 if packed else 0

        def head_scores(k, j):
            bank, col = (k % 2, j * NK) if packed else (j % 2, (j // 2) * NK)
            return scores_banks[:, bank, col:col + NK]

        pt_bank, out_bank, qk_bank, v_bank, y_bank, h_bank = (bank(x) for x in ("pt", "out", "qk", "v", "y", "h"))
        qk_banks = (qk_bank, v_bank) if small else (qk_bank, qk_bank)
        if small:
            v_bank = h_bank
        s_ctx_high = sem("ctx_high")
        s_ctx_split = sem("ctx_split")
        s_v = sem("v_ready")
        norm = Norm(m, ctx, tag, h_bank, (lambda n: (s_v, (n - 1) * PAIR)) if small else
                    (lambda n: (s_ctx_split, n)) if cross else (lambda n: (s_ctx_split, 0)),
                    params, weights)
        if small:
            qstack = [sb(f"qstack{i}", [P, TILES, PAIR * P], F32R) for i in range(2)]
            kstack = sb("kstack", [P, TILES, PAIR * NK], F32R)
            kblocks = [sb(f"kblocks{i}", [P, TILES, PAIR, GROUP * NK], F32R) for i in range(2)]
            qk_high = [m.wparts[i][0][:, TILES * P:TILES * P + 512] for i in range(2)]
        else:
            qk = [sb(f"qk{i}", [P, TILES, PAIR * P + PAIR * NK * (2 if cross else 1)]) for i in range(2)]
        VW = 32 if small else dh
        v = [sb(f"v{i}", [P, HEADS, VW]) for i in range(4)]
        probs = [sb(f"probs{i}", [P, GROUP, NK]) for i in range(4)]
        negmax = [sb(f"negmax{i}", [P, GROUP]) for i in range(4)]
        sums = [sb(f"sums{i}", [P, GROUP]) for i in range(4)]
        rsums = [sb(f"rsums{i}", [P, GROUP]) for i in range(4)]
        probsT = [sb(f"probsT{i}", [P, GROUP, P]) for i in range(2)]
        OT = 1 if small else 2
        outT = [sb(f"outT{i}", [P, OT * P]) for i in range(2)]
        if cross:
            ctx_in = [sb(f"ctx_in{i}", [P, PAIR, CTX_D]) for i in range(2)]
            ctx_high = [sb(f"ctx_high{i}", [P, PAIR * NK], F32R) for i in range(2)]
            ctx_low = [sb(f"ctx_low{i}", [P, PAIR * NK], F32R) for i in range(2)]

        s_ctx = [sem(f"ctx_in{i}") for i in range(2)]
        s_ctxT = sem("ctxT")
        s_scores = sem("scores")
        s_negmax = sem("negmax_ready")
        s_exp = sem("exp")
        s_rsums = sem("rsums_ready")
        s_probs = sem("probs_ready")
        s_pt = sem("pt")
        s_probsT = sem("probsT_ready")
        s_out = sem("heads_out")
        s_outT = sem("outT_ready")
        s_wo = sem("wo")
        s_resid = sem("resid")
        s_qkproj = sem("qkproj")
        s_qkhigh = sem("qkhigh")
        s_qk = sem("qk_ready")
        s_kblocks = [sem(f"kblocks{i}_ready") for i in range(2)]
        s_vproj = sem("vproj")
        s_zero = sem("zeroed")
        s_wo_clear = sem("wo_clear")
        s_wo_in = sem("wo_in")
        zeroed = ([[t[:] for t in kblocks[:1] + v], [kblocks[1][:]]] if small else
                  [[qk[0][:, :, PAIR * P:]], [qk[1][:, :, PAIR * P:]]] if cross else [[], []])
        ZEROED = (len(zeroed[0]), len(zeroed[0]) + len(zeroed[1]))
        weights.begin(ctx, tag, [] if small else [v[i][:].rearrange("p h d -> p (h d)") for i in range(4)])
        VN = PAIR if small else PSTEPS
        ctx.callback(m.end_stage)
        block = ctx.enter_context(nc.Block())

        number = lambda q, k: q * QSTEPS + k
        pair_of = lambda q, k: q * 2 + k // PSTEPS
        seq_of = lambda q, k: q * 4 + k // GROUPS

        def tile_at(q, k):
            s = k % PSTEPS
            if not live(pair_of(q, k) + 1, PAIRS):
                return None
            return s, (k // PSTEPS + 1) % 2, (pair_of(q, k) + 1) * PSTEPS + s

        def chunk_at(q, k):
            s = k % PSTEPS
            if not live(pair_of(q, k) + 1, PAIRS):
                return None
            if small:
                if s not in (PSTEPS - 2, PSTEPS - 1):
                    return None
                a, c = s - PSTEPS + 2, 0
            else:
                a, c = s // GROUPS, s % GROUPS
            return a, c, (2 * (k // PSTEPS + 1) + a) % 4, (pair_of(q, k) + 1) * VN + (a if small else s)

        def run(engine, step, prepare=lambda k: None):
            for k in range(-2 * PSTEPS, QSTEPS):
                step(0, k)
                if k < 0:
                    prepare(k + 2 * PSTEPS)
            with engine.Fori(1, QUADS - 1) as q:
                for k in range(QSTEPS):
                    step(q, k)
            for k in range(QSTEPS + 6):
                step(QUADS - 1, k)

        @block.sync
        def _(sp):
            def step(q, k):
                n, ahead = number(q, k), pair_of(q, k) + 2
                if cross and k % PSTEPS == 0 and live(ahead, PAIRS):
                    par = (k // PSTEPS) % 2
                    source = context(address(sp, q * 4 + 2 * (k // PSTEPS) + 4))
                    if due(ahead - 1):
                        sp.wait_ge(s_ctxT, ahead - 1)
                    sp.dma_start(ctx_in[par][0:NK, :, :], source).then_inc(s_ctx[par], 16)
                if small and k % PSTEPS == GROUPS and live(ahead - 1, PAIRS):
                    par = (k // PSTEPS + 1) % 2
                    if isinstance(n, int) and n <= GROUPS:
                        sp.wait_ge(s_zero, ZEROED[par])
                    if due((ahead - 1) * PSTEPS + GROUPS):
                        sp.wait_ge(s_qk, (ahead - 1) * PSTEPS + GROUPS)
                    for j in range(GROUP):
                        rows = slice(32 * j, 32 * j + 32)
                        sp.dma_start(kblocks[par][rows, :, :, j * NK:(j + 1) * NK].bitcast(F32),
                                     kstack[rows, :, :].bitcast(F32).rearrange("p t (a k) -> p t a k", a=PAIR)).then_inc(s_kblocks[par], 16)

            def prepare(k):
                if k == PSTEPS - 1:
                    weights.wait_split(sp)
                    following.sync_loads(sp, 0, following.early)
                    following.sync_params(sp)

            weights.sync_loads(sp, weights.early, len(weights.units))
            if small:
                sp.wait_ge(s_wo_clear, 1)
            for dst, src in wo_loads:
                sp.dma_start(dst, src).then_inc(s_wo_in, 16)
            run(sp, step, prepare)

        @block.gpsimd
        def _(pool):
            if small:
                nc.gpsimd.memset(wo_tiles, 0.0).then_inc(s_wo_clear, 1)

            def prepare(k):
                if k % PSTEPS == 3:
                    for t in zeroed[k // PSTEPS]:
                        nc.gpsimd.memset(t.bitcast(F32) if t.dtype == F32R else t, 0.0).then_inc(s_zero, 1)

            def step(q, k):
                n, s, ahead = number(q, k), k % PSTEPS, pair_of(q, k) + 2
                if s == 1 and live(ahead, PAIRS):
                    norm.gpsimd_rstd(pool, ahead)
                    norm.gpsimd_centre(pool, ahead, q * 4 + 2 * (k // PSTEPS) + 4)
                if s == 2 and live(ahead, PAIRS):
                    norm.gpsimd_h(pool, ahead)
                if s == 3 and live(ahead, PAIRS):
                    norm.gpsimd_bias(pool, ahead, q * 4 + 2 * (k // PSTEPS) + 4)
                if live(n - 1, STEPS):
                    i = (k - 1) % 4
                    if due(n):
                        pool.wait_ge(s_rsums, n)
                    nc.gpsimd.tensor_tensor(probs[i][:], probs[i][:], rsums[i][:].unsqueeze(2).broadcast_to([P, GROUP, NK]),
                                            ALU.mult).then_inc(s_probs, 1)

            run(pool, step, prepare)

        @block.scalar
        def _(act):
            def step(q, k):
                n, s, ahead = number(q, k), k % PSTEPS, pair_of(q, k) + 2
                tile = tile_at(q, k)
                if tile and small:
                    t, par, r = tile
                    width = PAIR * NK if t < GROUPS else PAIR * P
                    if due(r + 1):
                        act.wait_ge(s_qkproj, r + 1)
                    if due(r - 1):
                        act.wait_ge(s_qk, r - 1)
                    nc.scalar.copy(qk_high[t % 2][:, 0:width], qk_banks[k % 2][:, 0:width]).then_inc(s_qkhigh, 1)
                if live(n, STEPS):
                    i = k % 4
                    if due(n + 1):
                        act.wait_ge(s_negmax, n + 1)
                    if due(n - 3):
                        act.wait_ge(s_pt, n - 3)
                    for j in range(GROUP):
                        last = nc.scalar.activation(probs[i][:, j, :], head_scores(k, j), ACT.Exp,
                                                    bias=negmax[i][:, j:j + 1], scale=1.0, accum_out=sums[i][:, j:j + 1])
                    last.then_inc(s_exp, 1)
                if tile and not small:
                    t, par, r = tile
                    if due(r + 1):
                        act.wait_ge(s_qkproj, r + 1)
                    if due(n):
                        act.wait_ge(s_scores, n)
                    if cross:
                        if isinstance(n, int) and n <= 0:
                            act.wait_ge(s_zero, ZEROED[par])
                        nc.scalar.copy(qk[par][:, t, 0:PAIR * P], qk_bank[:, 0:PAIR * P])
                        for half in range(2):
                            rows = slice(half * dh, (half + 1) * dh)
                            last = nc.scalar.copy(
                                qk[par][rows, t, PAIR * P:].rearrange("p (a b k) -> p a b k", a=PAIR, b=2)[:, :, half, :],
                                qk_bank[rows, PAIR * P:PAIR * P + PAIR * NK].rearrange("p (a k) -> p a k", a=PAIR))
                        last.then_inc(s_qk, 1)
                    else:
                        nc.scalar.copy(qk[par][:, t, :], qk_bank[:, :]).then_inc(s_qk, 1)
                if small and live(n - 4, STEPS):
                    i = (k - 4) % 2
                    if due(n - 3):
                        act.wait_ge(s_out, n - 3)
                    if due(n - 5):
                        act.wait_ge(s_wo, n - 5)
                    nc.scalar.copy(outT[i][:], out_bank[:, 0:OT * P]).then_inc(s_outT, 1)
                chunk = chunk_at(q, k)
                if chunk:
                    a, c, slot, r = chunk
                    if due(r + 1):
                        act.wait_ge(s_vproj, r + 1)
                    if due((pair_of(q, k) - 1) * PSTEPS + (a + 1) * GROUPS):
                        act.wait_ge(s_out, (pair_of(q, k) - 1) * PSTEPS + (a + 1) * GROUPS)
                    if small:
                        if isinstance(n, int) and n < 0:
                            act.wait_ge(s_zero, ZEROED[0])
                        nc.scalar.copy(v[slot][0:NK, :, 0:dh], v_bank[0:NK, 0:inner].rearrange("p (h d) -> p h d", h=HEADS))\
                            .then_inc(s_v, 1)
                    else:
                        nc.scalar.copy(v[slot][0:NK, c * GROUP:(c + 1) * GROUP, :],
                                       v_bank[0:NK, 0:VCH].rearrange("p (h d) -> p h d", h=GROUP)).then_inc(s_v, 1)
                if s == 4 and live(ahead, PAIRS):
                    norm.scalar_affine(act, ahead, (k // PSTEPS) % 2, (s_vproj, (ahead - 1) * VN))
                if cross and s == 6 and live(ahead, PAIRS):
                    par = (k // PSTEPS) % 2
                    if due(ahead + 1):
                        act.wait_ge(s_ctxT, ahead + 1)
                    if due((ahead - 1) * VN):
                        act.wait_ge(s_vproj, (ahead - 1) * VN)
                    nc.scalar.copy(ctx_high[par][0:CTX_D, :], h_bank[0:CTX_D, 0:PAIR * NK]).then_inc(s_ctx_high, 1)

            def prepare(k):
                if k < len(weights.units):
                    weights.scalar_high(act, k)

            run(act, step, prepare)

        @block.vector
        def _(dve):
            def stack_tile(q, k):
                s, tile = k % PSTEPS, tile_at(q, k)
                if tile:
                    t, par, r = tile
                    if due(r + 1):
                        dve.wait_ge(s_qkhigh, r + 1)
                    if s == 0:
                        if due(16 * GROUP * half(q, k)):
                            dve.wait_ge(s_kblocks[(par + 1) % 2], 16 * GROUP * half(q, k))
                    width = PAIR * NK if t < GROUPS else PAIR * P
                    stack, minus = (kstack, m.minus_last8) if t < GROUPS else (qstack[par], m.minus_low8)
                    nc.vector.scalar_tensor_tensor(out=stack[:, t % GROUPS, :], in0=qk_high[t % 2][:, 0:width].bitcast(F32),
                                                   scalar=minus[:, 0:1], in1=qk_banks[k % 2][:, 0:width], op0=ALU.mult,
                                                   op1=ALU.add).then_inc(s_qk, 1)

            def step(q, k):
                n, s, ahead = number(q, k), k % PSTEPS, pair_of(q, k) + 2
                seq_ahead = q * 4 + 2 * (k // PSTEPS) + 4
                if small and s == 0:
                    stack_tile(q, k - 1)
                if s == 1 and live(ahead, PAIRS):
                    norm.wait_stats(dve, ahead)
                if live(n, STEPS):
                    if due(n + 1):
                        dve.wait_ge(s_scores, n + 1)
                    if due(n - 3):
                        dve.wait_ge(s_exp, n - 3)
                    if packed:
                        heads, best = scores_banks[:, k % 2, 0:GROUP * NK].rearrange("p (h k) -> p h k", h=GROUP), negmax[k % 4][:]
                    else:
                        heads = scores_banks[:, :, 0:2 * NK].rearrange("p b (c k) -> p b c k", c=2)
                        best = negmax[k % 4][:].rearrange("p (c b) -> p b c", b=2)
                    nc.vector.tensor_reduce(out=best, in_=heads, axis=AX.X, op=ALU.max, negate=True).then_inc(s_negmax, 1)
                if s == 1 and live(ahead, PAIRS):
                    norm.vector_moments(dve, ahead)
                if small and s != 0:
                    stack_tile(q, k - 1)
                if live(n - 1, STEPS):
                    i = (k - 1) % 4
                    if due(n):
                        dve.wait_ge(s_exp, n)
                    if due(n - 4):
                        dve.wait_ge(s_probs, n - 4)
                    nc.vector.reciprocal(rsums[i][:], sums[i][:]).then_inc(s_rsums, 1)
                if live(n - 3, STEPS):
                    i = (k - 3) % 2
                    if due(n - 2):
                        dve.wait_ge(s_pt, n - 2)
                    if due(n - 4):
                        dve.wait_ge(s_out, n - 4)
                    nc.vector.tensor_copy(probsT[i][0:NK, :, :], pt_bank[0:NK, :].rearrange("p (h k) -> p h k", h=GROUP))\
                        .then_inc(s_probsT, 1)
                if not small and live(n - 4, STEPS):
                    i = (k - 4) % 2
                    if due(n - 3):
                        dve.wait_ge(s_out, n - 3)
                    if due(n - 5):
                        dve.wait_ge(s_wo, n - 5)
                    nc.vector.tensor_copy(outT[i][:], out_bank[:, 0:OT * P]).then_inc(s_outT, 1)
                if live(n - 5, STEPS) and (k - 5) % GROUPS == GROUPS - 1:
                    seq = seq_of(q, k - 5)
                    if due(n - 4):
                        dve.wait_ge(s_wo, n - 4)
                    if due(pair_of(q, k - 5) + 1):
                        dve.wait_ge(norm.s_biased, pair_of(q, k - 5) + 1)
                    xt = m.x1(seq)
                    nc.vector.tensor_tensor(xt, y_bank[:, 0:D], xt, ALU.add).then_inc(s_resid, 1)
                if s == 0 and live(ahead, PAIRS):
                    norm.vector_stats(dve, ahead, seq_ahead)
                if s == 5 and live(ahead, PAIRS):
                    norm.vector_split(dve, ahead, (k // PSTEPS) % 2)
                if cross and s == 7 and live(ahead, PAIRS):
                    par = (k // PSTEPS) % 2
                    if due(ahead + 1):
                        dve.wait_ge(s_ctx_high, ahead + 1)
                    nc.vector.tensor_tensor(ctx_low[par][0:CTX_D, :], h_bank[0:CTX_D, 0:PAIR * NK],
                                            ctx_high[par][0:CTX_D, :].bitcast(F32), ALU.subtract).then_inc(s_ctx_split, 1)

            def half(q, k):
                return q + (k // PSTEPS + 1) // 2 if (k // PSTEPS + 1) % 2 == 0 else q + (k // PSTEPS + 1 + 1) // 2

            def prepare(k):
                if k < len(weights.units):
                    weights.vector_rest(dve, k)

            run(dve, step, prepare)

        @block.tensor
        def _(pe):
            def project(q, k):
                s, ahead = k % PSTEPS, pair_of(q, k) + 2
                tile = tile_at(q, k)
                if tile:
                    t, tpar, r = tile
                    if s == 0:
                        if due(ahead):
                            pe.wait_ge(norm.s_split, ahead)
                        if cross:
                            if due(ahead):
                                pe.wait_ge(s_ctx_split, ahead)
                    if due(r - 1 if small else r):
                        pe.wait_ge(s_qk, r - 1 if small else r)
                    cols = slice(t % TILES * P, (t % TILES + 1) * P)
                    (qh, ql, qs), (kh, kl, ks) = m.wparts[0], m.wparts[1]
                    hh, hl, hs = norm.high[tpar][:], norm.low[tpar][:], norm.stack[tpar][0:STACK, :]
                    if not small or t >= GROUPS:
                        last = products(nc, qk_banks[k % 2][:, 0:PAIR * P],
                                        [(qh[:, cols], hh), (qh[:, cols], hl), (ql[:, cols], hh), (qs[0:STACK, cols], hs)])
                    kcol = 0 if small else PAIR * P
                    kout = qk_banks[k % 2][:, kcol:kcol + PAIR * NK]
                    if small and t >= GROUPS:
                        pass
                    elif cross:
                        ch, cl = ctx_high[tpar][0:CTX_D, :], ctx_low[tpar][0:CTX_D, :]
                        last = products(nc, kout, [(kh[0:CTX_D, cols], ch), (kh[0:CTX_D, cols], cl), (kl[0:CTX_D, cols], ch)])
                    else:
                        last = products(nc, kout, [(kh[:, cols], hh), (kh[:, cols], hl), (kl[:, cols], hh), (ks[0:STACK, cols], hs)])
                    last.then_inc(s_qkproj, 1)

            def step(q, k):
                n, s, ahead = number(q, k), k % PSTEPS, pair_of(q, k) + 2
                a, grp = (k % PSTEPS) // GROUPS, k % GROUPS
                par = (k // PSTEPS) % 2
                if live(n, STEPS):
                    if due(n - SCORES_LAG):
                        pe.wait_ge(s_exp, n - SCORES_LAG)
                    if s == 0:
                        if small:
                            pe.wait_ge(s_kblocks[par], (q + 1) * (16 * GROUP))
                        pe.wait_ge(s_qk, (pair_of(q, k) + 1) * PSTEPS)
                    if small:
                        last = nc.tensor.matmul(scores_banks[:, k % 2, 0:GROUP * NK], qstack[par][:, grp, a * P:(a + 1) * P],
                                                kblocks[par][:, grp, a, :], start=True, stop=True)
                    elif cross:
                        for c in range(GROUP // 2):
                            t = 2 * grp + c
                            last = nc.tensor.matmul(scores_banks[:, k % 2, c * 2 * NK:(c + 1) * 2 * NK], qk[par][:, t, a * P:(a + 1) * P],
                                                    qk[par][:, t, PAIR * P + a * 2 * NK:PAIR * P + (a + 1) * 2 * NK],
                                                    start=True, stop=True)
                    else:
                        for j in range(GROUP):
                            rows, t = slice(dh * (j % 2), dh * (j % 2) + dh), 2 * grp + j // 2
                            last = nc.tensor.matmul(head_scores(k, j), qk[par][rows, t, a * P:(a + 1) * P],
                                                    qk[par][rows, t, PAIR * P + a * NK:PAIR * P + (a + 1) * NK], start=True, stop=True)
                    last.then_inc(s_scores, 1)
                project(q, k)
                if live(n - 3, STEPS):
                    if due(n - 2):
                        pe.wait_ge(s_probs, n - 2)
                    if due(n - 3):
                        pe.wait_ge(s_probsT, n - 3)
                    for j in range(GROUP):
                        last = nc.tensor.transpose(pt_bank[0:NK, j * P:(j + 1) * P], probs[(k - 3) % 4][:, j, :], m.ident[:])
                    last.then_inc(s_pt, 1)
                chunk = chunk_at(q, k)
                if chunk:
                    ca, c, slot, r = chunk
                    tpar = (k // PSTEPS + 1) % 2
                    if due(r):
                        pe.wait_ge(s_v, r)
                    if small and ca == 0 and live(ahead, PAIRS):
                        if cross:
                            pe.wait_ge(s_ctx_split, ahead + 1)
                        else:
                            pe.wait_ge(norm.s_y, ahead * 2 + 2)
                    cols = slice(c * VCH, (c + 1) * VCH)
                    vh, vl, vs = m.wparts[2]
                    if cross:
                        tok = slice(ca * NK, (ca + 1) * NK)
                        ch, cl = ctx_high[tpar][0:CTX_D, tok], ctx_low[tpar][0:CTX_D, tok]
                        last = products(nc, v_bank[0:NK, 0:VCH],
                                        [(ch, vh[0:CTX_D, cols]), (ch, vl[0:CTX_D, cols]), (cl, vh[0:CTX_D, cols])])
                    else:
                        tok = slice(ca * P, (ca + 1) * P)
                        hh, hl, hs = norm.high[tpar][:, tok], norm.low[tpar][:, tok], norm.stack[tpar][0:STACK, tok]
                        last = products(nc, v_bank[:, 0:VCH],
                                        [(hh, vh[:, cols]), (hh, vl[:, cols]), (hl, vh[:, cols]), (hs, vs[0:STACK, cols])])
                    last.then_inc(s_vproj, 1)
                if live(n - 4, STEPS):
                    if due(n - 3):
                        pe.wait_ge(s_probsT, n - 3)
                    if due(n - 4):
                        pe.wait_ge(s_outT, n - 4)
                    g3, slot = (k - 4) % GROUPS, ((k - 4) // GROUPS) % 4
                    if g3 == 0:
                        if small:
                            pe.wait_ge(s_v, seq_of(q, k - 4) + 1)
                        else:
                            pe.wait_ge(s_v, (seq_of(q, k - 4) + 1) * GROUPS)
                    for j in range(GROUP):
                        rows, col = (32 * j, 0) if small else (dh * (j % 2), j // 2)
                        last = nc.tensor.matmul(out_bank[rows:rows + VW, col * P:(col + 1) * P], v[slot][0:NK, g3 * GROUP + j, :],
                                                probsT[(k - 4) % 2][0:NK, j, :], start=True, stop=True)
                    last.then_inc(s_out, 1)
                if live(n - 5, STEPS):
                    g4 = (k - 5) % GROUPS
                    if due(n - 4):
                        pe.wait_ge(s_outT, n - 4)
                    if isinstance(n, int) and n == 5:
                        pe.wait_ge(s_wo_in, 16 * len(wo_loads))
                    if g4 == 0:
                        if due(seq_of(q, k - 5)):
                            pe.wait_ge(s_resid, seq_of(q, k - 5))
                    for t in range(OT):
                        last = nc.tensor.matmul(y_bank[:, 0:D], outT[(k - 5) % 2][:, t * P:(t + 1) * P], m.wo[:, g4 * OT + t, :],
                                                start=(g4 == 0 and t == 0), stop=(g4 == GROUPS - 1 and t == OT - 1))
                    last.then_inc(s_wo, 1)
                if s == 4 and live(ahead, PAIRS):
                    norm.tensor_transpose(pe, ahead)
                if cross and s == 6 and live(ahead, PAIRS):
                    cpar = (k // PSTEPS) % 2
                    if due(ahead * 2 + 2):
                        pe.wait_ge(norm.s_y, ahead * 2 + 2)
                    pe.wait_ge(s_ctx[cpar], (q + (k // PSTEPS + 2) // 2 + 1) * 16 if cpar == 0 else (q + (k // PSTEPS + 1) // 2 + 1) * 16)
                    for b2 in range(PAIR):
                        last = nc.tensor.transpose(h_bank[0:CTX_D, b2 * NK:(b2 + 1) * NK], ctx_in[cpar][0:NK, b2, :], m.ident[0:NK, 0:NK])
                    last.then_inc(s_ctxT, 1)

            def prepare(k):
                if k == PSTEPS - 1:
                    weights.wait_split(pe)

            run(pe, step, prepare)


def feed_forward_weights(m, number, params, g, b, w1, b1, b2):
    return Weights(m, number, [(w1, m.wparts[0], 2 * FF, 1.0, False)], params.loads(g, b, b2, b1))


def feed_forward(m, tag, gelu, w2, params, weights, following=None, out=None):
    nc, bias1 = m.nc, params.bias1
    TILES = FF // P
    with ExitStack() as ctx:
        sb = lambda name, shape, dt=F32: ctx.enter_context(nc.sbuf_tensor(f"{tag}_{name}", shape, dt))
        sem = lambda name: m.semaphore(ctx, f"{tag}_{name}")
        bank = lambda name: ctx.enter_context(nc.psum_tensor(f"{tag}_{name}_bank", [P, 512], F32))
        up_bank = [bank(f"up{i}") for i in range(2)]
        y_bank = [[bank(f"y{i}{a}") for a in range(PAIR)] for i in range(2)]
        h_bank = bank("h")
        norm = Norm(m, ctx, tag, h_bank, lambda n: (None, 0), params, weights)
        gate = [sb(f"gate{i}", [P, PAIR * P]) for i in range(2)]
        act_t = [sb(f"hidden{i}", [P, PAIR * P]) for i in range(2)]
        s_up = sem("up")
        s_gate = sem("gate_ready")
        s_hidden = sem("hidden_ready")
        s_down = sem("down")
        s_resid = sem("resid")
        s_store = sem("store")
        s_w2_in = sem("w2_in")
        spare = sb("rem_high", [P, STAGE_WIDE])
        weights.begin(ctx, tag, [spare[:]])
        ctx.callback(m.end_stage)
        block = ctx.enter_context(nc.Block())
        BODY = 2 * TILES
        number = lambda q, k: q * BODY + k
        pair_of = lambda q, k: q * 2 + k // TILES
        TOTAL = PAIRS * TILES

        def run(engine, step, prepare=lambda k: None):
            for k in range(-2 * TILES, BODY):
                step(0, k)
                if k < 0:
                    prepare(k + 2 * TILES)
            with engine.Fori(1, QUADS - 1) as q:
                for k in range(BODY):
                    step(q, k)
            for k in range(BODY + 4):
                step(QUADS - 1, k)

        @block.sync
        def _(sp):
            sp.dma_start(m.wo[:, 0:TILES, :], w2.rearrange("(t p) n -> p t n", p=P)).then_inc(s_w2_in, 16)
            if following:
                weights.wait_split(sp)
                following.sync_loads(sp, 0, following.early)
                following.sync_params(sp)
            if out is None:
                return

            def step(q, k):
                n = number(q, k)
                if (k - 3) % TILES == TILES - 1 and live(n - 3, TOTAL):
                    seq = address(sp, q * 4 + 2 * ((k - 3) // TILES))
                    if due(pair_of(q, k - 3) + 1):
                        sp.wait_ge(s_resid, pair_of(q, k - 3) + 1)
                    sp.dma_start(out[bass.ds(seq, PAIR), :, :].rearrange("s p d -> p s d"), m.xpair(seq)).then_inc(s_store, 16)

            run(sp, step)
            sp.wait_ge(s_store, 16 * PAIRS)

        @block.gpsimd
        def _(pool):
            def step(q, k):
                s, ahead = k % TILES, pair_of(q, k) + 2
                if live(ahead, PAIRS):
                    if s == 1:
                        norm.gpsimd_rstd(pool, ahead)
                        norm.gpsimd_centre(pool, ahead, q * 4 + 2 * (k // TILES) + 4)
                    if s == 2:
                        norm.gpsimd_h(pool, ahead)
                    if s == 4:
                        norm.gpsimd_bias(pool, ahead, q * 4 + 2 * (k // TILES) + 4)

            run(pool, step)

        @block.scalar
        def _(act):
            def step(q, k):
                n, s, ahead = number(q, k), k % TILES, pair_of(q, k) + 1
                if live(n, TOTAL):
                    if due(n + 1):
                        act.wait_ge(s_up, n + 1)
                    if due(n - 1):
                        act.wait_ge(s_hidden, n - 1)
                    nc.scalar.activation(gate[k % 2][:], up_bank[k % 2][:, PAIR * P:], gelu,
                                         bias=bias1[:, TILES + s:TILES + s + 1], scale=1.0).then_inc(s_gate, 1)
                if s == 1 and live(ahead, PAIRS):
                    norm.scalar_affine(act, ahead, (k // TILES + 1) % 2, (s_up, (ahead - 1) * TILES))

            def prepare(k):
                if k < len(weights.units):
                    weights.scalar_high(act, k)

            run(act, step, prepare)

        @block.vector
        def _(dve):
            def step(q, k):
                n, s, ahead = number(q, k), k % TILES, pair_of(q, k) + 2
                seq_ahead = q * 4 + 2 * (k // TILES) + 4
                if s == 1 and live(ahead, PAIRS):
                    norm.wait_stats(dve, ahead)
                if live(n, TOTAL):
                    if due(n + 1):
                        dve.wait_ge(s_gate, n + 1)
                    if due(n - 1):
                        dve.wait_ge(s_down, n - 1)
                    nc.vector.scalar_tensor_tensor(out=act_t[k % 2][:], in0=up_bank[k % 2][:, 0:PAIR * P],
                                                   scalar=bias1[:, s:s + 1], in1=gate[k % 2][:], op0=ALU.add,
                                                   op1=ALU.mult).then_inc(s_hidden, 1)
                if (k - 3) % TILES == TILES - 1 and live(n - 3, TOTAL):
                    seq, ypar = q * 4 + 2 * ((k - 3) // TILES), ((k - 3) // TILES) % 2
                    if due(n - 2):
                        dve.wait_ge(s_down, n - 2)
                    if due(pair_of(q, k - 3) + 1):
                        dve.wait_ge(norm.s_biased, pair_of(q, k - 3) + 1)
                    for a in range(PAIR):
                        xt = m.xs(seq, a)
                        last = nc.vector.tensor_tensor(xt, y_bank[ypar][a][:, 0:D], xt, ALU.add)
                    last.then_inc(s_resid, 1)
                if live(ahead, PAIRS):
                    if s == 0:
                        norm.vector_stats(dve, ahead, seq_ahead)
                    if s == 1:
                        norm.vector_moments(dve, ahead)
                if s == 2 and live(ahead - 1, PAIRS):
                    norm.vector_split(dve, ahead - 1, (k // TILES + 1) % 2)

            def prepare(k):
                if k < len(weights.units):
                    weights.vector_rest(dve, k)

            run(dve, step, prepare)

        @block.tensor
        def _(pe):
            def step(q, k):
                n, s, ahead = number(q, k), k % TILES, pair_of(q, k) + 1
                par = (k // TILES) % 2
                if live(n, TOTAL):
                    if s == 0:
                        pe.wait_ge(norm.s_split, pair_of(q, k) + 1)
                    if due(n - 1):
                        pe.wait_ge(s_hidden, n - 1)
                    wh, wl, ws = m.wparts[0]
                    hh, hl, hs = norm.high[par][:], norm.low[par][:], norm.stack[par][0:STACK, :]
                    for half in range(2):
                        cols = slice(half * FF + s * P, half * FF + (s + 1) * P)
                        last = products(nc, up_bank[k % 2][:, half * PAIR * P:(half + 1) * PAIR * P],
                                        [(wh[:, cols], hh), (wh[:, cols], hl), (wl[:, cols], hh), (ws[0:STACK, cols], hs)])
                    last.then_inc(s_up, 1)
                if live(n - 2, TOTAL):
                    t, ypar = (k - 2) % TILES, ((k - 2) // TILES) % 2
                    if due(n - 1):
                        pe.wait_ge(s_hidden, n - 1)
                    if t == 0:
                        if due(pair_of(q, k - 2) - 1):
                            pe.wait_ge(s_resid, pair_of(q, k - 2) - 1)
                    for a in range(PAIR):
                        last = nc.tensor.matmul(y_bank[ypar][a][:, 0:D], act_t[k % 2][:, a * P:(a + 1) * P], m.wo[:, t, :],
                                                start=(t == 0), stop=(t == TILES - 1))
                    last.then_inc(s_down, 1)
                if s == 0 and live(ahead, PAIRS):
                    norm.tensor_transpose(pe, ahead)

            def prepare(k):
                if k == 2 * TILES - 1:
                    weights.wait_split(pe)
                    pe.wait_ge(s_w2_in, 16)

            run(pe, step, prepare)


def build(nc, A, out):
    m = Machine(nc)
    with ExitStack() as ctx:
        m.ctx = ctx
        sb = lambda name, shape, dt=F32: ctx.enter_context(nc.sbuf_tensor(name, shape, dt))
        m.x = sb("x_tokens", [P, SEQS * D])
        m.wparts = [[sb(f"w{i}_{part}", [P, 1280], F32R) for part in ("high", "low", "stack")] for i in range(3)]
        m.wo = sb("w_out", [P, 10, D])
        m.staging = [sb(f"staging{i}", [P, STAGE_WIDE]) for i in range(4)]
        params = [Params(sb, i) for i in range(2)]
        m.ident = sb("ident", [P, P])
        m.eps = sb("eps", [P, PAIR])
        m.minus_half = sb("minus_half", [P, PAIR])
        m.minus_low_row = sb("minus_low_row", [P, 1])
        m.minus_last_row = sb("minus_last_row", [P, 1])
        m.minus_low8 = sb("minus_low8", [P, 1])
        m.minus_last8 = sb("minus_last8", [P, 1])
        band = sb("band", [P, 2, GROUP])
        m.x1 = lambda seq: m.x[:, bass.ds(seq * D, D)]
        m.xs = lambda seq, a: m.x[:, bass.ds(seq * D + a * D, D)]
        m.xpair = lambda seq: m.x[:, bass.ds(seq * D, PAIR * D)].rearrange("p (a d) -> p a d", a=PAIR)

        x_in, c_in = A["x"], A["ctx_768"]
        context = lambda seq: c_in[bass.ds(seq, PAIR), :, :].rearrange("s p d -> p s d")
        L0 = lambda name: A["L0_xattn_" + name]
        L1 = lambda name: A["L1_xattn_" + name]
        weights = [
            attention_weights(m, 0, 8, params[0], L0("n1_g"), L0("n1_b"), L0("q1"), L0("k1"), L0("v1"), L0("o1_b")),
            attention_weights(m, 1, 8, params[1], L0("n2_g"), L0("n2_b"), L0("q2"), L0("k2"), L0("v2"), L0("o2_b")),
            feed_forward_weights(m, 2, params[0], L0("n3_g"), L0("n3_b"), L0("ff_w1"), L0("ff_b1"), L0("ff_b2")),
            attention_weights(m, 3, 64, params[1], L1("g1"), L1("be1"), L1("wq1"), L1("wk1"), L1("wv1"), L1("bo1")),
            attention_weights(m, 4, 64, params[0], L1("g2"), L1("be2"), L1("wq2"), L1("wk2"), L1("wv2"), L1("bo2")),
            feed_forward_weights(m, 5, params[1], L1("g3"), L1("be3"), L1("w_ff1"), L1("b_ff1"), L1("b_ff2"))]
        CHUNK = 2 * PAIR
        s_tokens_first = ctx.enter_context(nc.semaphore("tokens_first"))
        s_tokens_rest = ctx.enter_context(nc.semaphore("tokens_rest"))
        m.tokens_wanted = ((s_tokens_first, 16), (s_tokens_rest, 16 * (SEQS // CHUNK - 1)))

        with ExitStack() as c0:
            s_pool = m.semaphore(c0, "const_pool")
            c0.callback(m.end_stage)
            block = c0.enter_context(nc.Block())

            @block.sync
            def _(sp):
                for i in range(SEQS // CHUNK):
                    sp.dma_start(m.x[:, i * CHUNK * D:(i + 1) * CHUNK * D].rearrange("p (s d) -> p s d", d=D),
                                 x_in[i * CHUNK:(i + 1) * CHUNK, :, :].rearrange("s p d -> p s d"))\
                        .then_inc(s_tokens_rest if i else s_tokens_first, 16)
                    if i == 0:
                        weights[0].sync_params(sp)
                        weights[0].sync_loads(sp, 0, weights[0].early)

            @block.gpsimd
            def _(pool):
                made = [0]

                def link(instruction):
                    made[0] += 1
                    instruction.then_inc(s_pool, 1)
                    pool.wait_ge(s_pool, made[0])

                link(nc.gpsimd.memset(m.ident[:], 0.0))
                link(nc.gpsimd.affine_select(out=m.ident[:], in_=m.ident[:], compare_op=ALU.not_equal, fill=1.0, base=0,
                                             pattern=[[-1, P]], channel_multiplier=1))
                link(nc.gpsimd.memset(m.minus_half[:], -0.5))
                link(nc.gpsimd.memset(m.eps[:], EPS))
                for tile, row in ((m.minus_low_row, 1), (m.minus_last_row, 2)):
                    link(nc.gpsimd.memset(tile[:], 0.0))
                    link(nc.gpsimd.memset(tile[row * REM:(row + 1) * REM, :], -1.0))
                link(nc.gpsimd.memset(band[:], -1.0))
                for i in range(2):
                    lo = 8 * (i + 1)
                    link(nc.gpsimd.affine_select(out=band[:, i, :], in_=band[:, i, :], compare_op=ALU.is_ge, fill=0.0, base=-lo,
                                                 pattern=[[-32, GROUP]], channel_multiplier=1))
                    link(nc.gpsimd.affine_select(out=band[:, i, :], in_=band[:, i, :], compare_op=ALU.is_ge, fill=0.0,
                                                 base=lo + 7, pattern=[[32, GROUP]], channel_multiplier=-1))

            @block.vector
            def _(dve):
                dve.wait_ge(s_pool, 13)
                for i, tile in enumerate((m.minus_low8, m.minus_last8)):
                    nc.vector.tensor_reduce(out=tile[:], in_=band[:, i, :], axis=AX.X, op=ALU.add)

        attention(m, "a0", 8, False, L0("o1_w"), context, params[0], weights[0], weights[1])
        m.tokens_wanted = None
        attention(m, "c0", 8, True, L0("o2_w"), context, params[1], weights[1], weights[2])
        feed_forward(m, "f0", ACT.Gelu, L0("ff_w2"), params[0], weights[2], weights[3])
        attention(m, "a1", 64, False, L1("wo1"), context, params[1], weights[3], weights[4])
        attention(m, "c1", 64, True, L1("wo2"), context, params[0], weights[4], weights[5])
        feed_forward(m, "f1", ACT.Gelu_apprx_tanh, L1("w_ff2"), params[1], weights[5], out=out)


def kernel(**inputs):
    import concourse.bacc as bacc
    from concourse.bass_utils import run_bass_kernel_spmd

    nc = bacc.Bacc("TRN2", target_bir_lowering=False, num_devices=1)
    arrays, A = {}, {}
    for name, value in inputs.items():
        a = np.ascontiguousarray(value)
        arrays[f"in_{name}"] = a
        A[name] = nc.dram_tensor(f"in_{name}", a.shape, mybir.dt.from_np(a.dtype), kind="ExternalInput").ap()
    out = nc.dram_tensor("out_x", (SEQS, TOK, D), F32, kind="ExternalOutput").ap()
    build(nc, A, out)
    result = run_bass_kernel_spmd(nc, [arrays], core_ids=[0])
    return result.results[0]["out_x"]
```
